# Optimizing a Trainium2 kernel written in Bass

```python
import numpy as np
import jax
import jax.numpy as jnp

def _softmax(x, axis=-1):
    return jax.nn.softmax(x, axis=axis)

def _gelu(x):
    return jax.nn.gelu(x, approximate=True)

def _silu(x):
    return jax.nn.silu(x)

def _sigmoid(x):
    return jax.nn.sigmoid(x)

def _layernorm(x, axis=-1, eps=1e-05):
    m = jnp.mean(x, axis=axis, keepdims=True)
    v = jnp.var(x, axis=axis, keepdims=True)
    return (x - m) / jnp.sqrt(v + eps)

def _scatter_add(tgt, idx, src, axis=0):
    return tgt.at[idx].add(src)

def _segment_sum(src, seg, n):
    return jax.ops.segment_sum(src, seg, n)
kernel_name = 'mk_xattn_ffn_d2_seqx_r4_4f2d9f'

def setup_inputs(seed: int=0):
    np.random.seed(seed)
    _w = jnp.asarray

    def _rec_inputs():
        import jax
        import jax.numpy as jnp
        _rk = jax.random.key(seed)
        x = 7.22e-05 + 1 * jax.random.normal(jax.random.fold_in(_rk, 1), (32, 256, 256), jnp.float32)
        _lenS = 256 - jax.random.randint(jax.random.fold_in(_rk, 7), (32,), 0, max(1, 256 // 4) + 1, jnp.int32)
        _lenS2 = 256 - jax.random.randint(jax.random.fold_in(_rk, 8), (32,), 0, max(1, 256 // 4) + 1, jnp.int32)
        _ctx_1024P = jax.random.normal(jax.random.fold_in(_rk, 11), (32, 16, 256), jnp.float32)
        _ctx_1024c = jax.random.dirichlet(jax.random.fold_in(_rk, 511), 0.3 * jnp.ones((16,), jnp.float32), (32, 256))
        _ctx_1024t = jnp.einsum('bsk,bkd->bsd', _ctx_1024c, _ctx_1024P)
        _ctx_1024t = _ctx_1024t * jax.lax.rsqrt(jnp.mean(jnp.square(_ctx_1024t)) + 1e-12) * 0.953939
        ctx_1024 = 4.13588e-05 + 0.999923 * (_ctx_1024t + 0.3 * jax.random.normal(jax.random.fold_in(_rk, 611), (32, 256, 256), jnp.float32))
        _validS = jnp.arange(256)[None, :] < _lenS[:, None]
        _validS2 = jnp.arange(256)[None, :] < _lenS2[:, None]
        _causal = jnp.tril(jnp.ones((256, 256), dtype=bool))
        mask_Bx1xS2_ik0 = jnp.where(jnp.broadcast_to(_validS2[:, None, :], (32, 1, 256)), 0, 1).astype(jnp.int32)
        return (x, ctx_1024, mask_Bx1xS2_ik0)
    x, ctx_1024, mask_Bx1xS2_ik0 = _rec_inputs()

    def _L0_xattn_setup():
        import jax, jax.numpy as jnp
        import numpy as np
        D_MODEL = 256
        HEADS = 16
        D_HEAD = D_MODEL // HEADS
        SEQ = 512
        C = 2
        K_TOP = int(C * np.log(SEQ))
        key = jax.random.key(seed)
        ks = jax.random.split(key, 5)
        s = 0.02
        return {'Q': jax.random.normal(ks[0], (4, SEQ, D_MODEL), jnp.float32), 'K': jax.random.normal(ks[1], (4, SEQ, D_MODEL), jnp.float32), 'V': jax.random.normal(ks[2], (4, SEQ, D_MODEL), jnp.float32), 'Wq': jax.random.normal(ks[3], (D_MODEL, D_HEAD), jnp.float32) * s, 'bq': jnp.zeros((D_HEAD,), jnp.float32), 'Wout': jax.random.normal(ks[4], (HEADS * D_HEAD, D_MODEL), jnp.float32) * s, 'bout': jnp.zeros((D_MODEL,), jnp.float32)}
    _L0_xattn_all = _L0_xattn_setup()
    _L0_xattn_in = {k: v for k, v in _L0_xattn_all.items() if k in ('Wq', 'bq', 'Wout', 'bout')}
    del _L0_xattn_all

    def _L0_ffn_setup():
        import jax, jax.numpy as jnp
        import numpy as np
        B, S, D, E = (2, 512, 256, 8)
        key = jax.random.key(seed)
        ks = jax.random.split(key, 5)
        x = jax.random.normal(ks[0], (B, S, D), dtype=jnp.float32)
        router_w = jax.random.normal(ks[1], (E, D), dtype=jnp.float32) * 0.02
        router_b = jnp.zeros((E,), dtype=jnp.float32)
        expert_w = jax.random.normal(ks[2], (E, D, D), dtype=jnp.float32) * 0.02
        expert_b = jnp.zeros((E, D), dtype=jnp.float32)
        return {'x': x, 'router_w': router_w, 'router_b': router_b, 'expert_w': expert_w, 'expert_b': expert_b}
    _L0_ffn_all = _L0_ffn_setup()
    _L0_ffn_in = {k: v for k, v in _L0_ffn_all.items() if k in ('router_w', 'router_b', 'expert_w', 'expert_b')}
    del _L0_ffn_all

    def _L1_xattn_setup():
        import jax, jax.numpy as jnp
        import numpy as np
        H = 16
        D_MODEL = 256
        D_K = D_MODEL // H
        NEG = -1000000000.0

        def _split_heads(x, B, S):
            return x.reshape(B, S, H, D_K).transpose(0, 2, 1, 3)
        key = jax.random.key(seed)
        ks = jax.random.split(key, 13)
        B, S = (2, 512)
        std = 1.0 / np.sqrt(D_MODEL)
        inp = {'query': jax.random.normal(ks[0], (B, S, D_MODEL), jnp.float32), 'key': jax.random.normal(ks[1], (B, S, D_MODEL), jnp.float32), 'value': jax.random.normal(ks[2], (B, S, D_MODEL), jnp.float32), 'mask': jax.random.randint(ks[3], (B, 1, S), 0, 2, jnp.int32), 'Wq': jax.random.normal(ks[4], (D_MODEL, D_MODEL), jnp.float32) * std, 'bq': jax.random.normal(ks[5], (D_MODEL,), jnp.float32) * std, 'Wk': jax.random.normal(ks[6], (D_MODEL, D_MODEL), jnp.float32) * std, 'bk': jax.random.normal(ks[7], (D_MODEL,), jnp.float32) * std, 'Wv': jax.random.normal(ks[8], (D_MODEL, D_MODEL), jnp.float32) * std, 'bv': jax.random.normal(ks[9], (D_MODEL,), jnp.float32) * std, 'Wo': jax.random.normal(ks[10], (D_MODEL, D_MODEL), jnp.float32) * std, 'bo': jax.random.normal(ks[11], (D_MODEL,), jnp.float32) * std}
        return inp
    _L1_xattn_all = _L1_xattn_setup()
    _L1_xattn_in = {k: v for k, v in _L1_xattn_all.items() if k in ('Wq', 'bq', 'Wk', 'bk', 'Wv', 'bv', 'Wo', 'bo')}
    del _L1_xattn_all

    def _L1_ffn_setup():
        import jax, jax.numpy as jnp
        import numpy as np
        HIDDEN = 256
        INNER = 1024

        def _weight_quant(w):
            scale = 1.0 / jnp.clip(jnp.mean(jnp.abs(w)), 1e-05)
            wq = jnp.clip(jnp.round(w * scale), -1.0, 1.0) / scale
            return w + jax.lax.stop_gradient(wq - w)

        def _act_quant(x):
            scale = 127.0 / jnp.clip(jnp.max(jnp.abs(x), axis=-1, keepdims=True), 1e-05)
            xq = jnp.clip(jnp.round(x * scale), -128.0, 127.0) / scale
            return x + jax.lax.stop_gradient(xq - x)

        def _bitlinear(x, w):
            return jnp.einsum('bsi,oi->bso', _act_quant(x), _weight_quant(w))
        key = jax.random.key(seed)
        k0, k1, k2, k3 = jax.random.split(key, 4)
        x = jax.random.normal(k0, (4, 512, HIDDEN), dtype=jnp.float32)
        w_gate = jax.random.normal(k1, (INNER, HIDDEN), dtype=jnp.float32) / np.sqrt(HIDDEN)
        w_up = jax.random.normal(k2, (INNER, HIDDEN), dtype=jnp.float32) / np.sqrt(HIDDEN)
        w_down = jax.random.normal(k3, (HIDDEN, INNER), dtype=jnp.float32) / np.sqrt(INNER)
        return {'x': x, 'w_gate': w_gate, 'w_up': w_up, 'w_down': w_down}
    _L1_ffn_all = _L1_ffn_setup()
    _L1_ffn_in = {k: v for k, v in _L1_ffn_all.items() if k in ('w_gate', 'w_up', 'w_down')}
    del _L1_ffn_all
    return {'x': x, 'ctx_1024': ctx_1024, 'mask_Bx1xS2_ik0': mask_Bx1xS2_ik0, 'L0_xattn_Wq': _L0_xattn_in['Wq'], 'L0_xattn_bq': _L0_xattn_in['bq'], 'L0_xattn_Wout': _L0_xattn_in['Wout'], 'L0_xattn_bout': _L0_xattn_in['bout'], 'L0_ffn_router_w': _L0_ffn_in['router_w'], 'L0_ffn_router_b': _L0_ffn_in['router_b'], 'L0_ffn_expert_w': _L0_ffn_in['expert_w'], 'L0_ffn_expert_b': _L0_ffn_in['expert_b'], 'L1_xattn_Wq': _L1_xattn_in['Wq'], 'L1_xattn_bq': _L1_xattn_in['bq'], 'L1_xattn_Wk': _L1_xattn_in['Wk'], 'L1_xattn_bk': _L1_xattn_in['bk'], 'L1_xattn_Wv': _L1_xattn_in['Wv'], 'L1_xattn_bv': _L1_xattn_in['bv'], 'L1_xattn_Wo': _L1_xattn_in['Wo'], 'L1_xattn_bo': _L1_xattn_in['bo'], 'L1_ffn_w_gate': _L1_ffn_in['w_gate'], 'L1_ffn_w_up': _L1_ffn_in['w_up'], 'L1_ffn_w_down': _L1_ffn_in['w_down']}

def reference(x, ctx_1024, mask_Bx1xS2_ik0, L0_xattn_Wq, L0_xattn_bq, L0_xattn_Wout, L0_xattn_bout, L0_ffn_router_w, L0_ffn_router_b, L0_ffn_expert_w, L0_ffn_expert_b, L1_xattn_Wq, L1_xattn_bq, L1_xattn_Wk, L1_xattn_bk, L1_xattn_Wv, L1_xattn_bv, L1_xattn_Wo, L1_xattn_bo, L1_ffn_w_gate, L1_ffn_w_up, L1_ffn_w_down):
    import jax
    import jax.numpy as jnp

    def _L0_xattn_ref(Q, K, V, Wq, bq, Wout, bout):
        import jax, jax.numpy as jnp
        import numpy as np
        D_MODEL = 256
        HEADS = 16
        D_HEAD = D_MODEL // HEADS
        SEQ = 512
        C = 2
        K_TOP = int(C * np.log(SEQ))
        B, L, _ = Q.shape
        q = (Q @ Wq + bq).transpose(0, 2, 1)
        k_ = (K @ Wq + bq).transpose(0, 2, 1)
        v = (V @ Wq + bq).transpose(0, 2, 1)
        Qf = jnp.fft.fft(q.astype(jnp.complex64))
        Kf = jnp.fft.fft(k_.astype(jnp.complex64))
        corr = jnp.real(jnp.fft.ifft(Qf * jnp.conj(Kf)))
        corr = corr.mean(axis=(0, 1))
        W_topk, I_topk = jax.lax.top_k(corr, K_TOP)
        W_topk = jax.nn.softmax(W_topk)

        def body(R, ws):
            w, shift = ws
            return (R + w * jnp.roll(v, -shift, axis=-1), None)
        R3, _ = jax.lax.scan(body, jnp.zeros_like(v), (W_topk, I_topk))
        R = jnp.broadcast_to(R3[:, None], (B, HEADS, D_HEAD, L)).reshape(B, L, HEADS * D_HEAD)
        return R @ Wout + bout

    def _L0_ffn_ref(x, router_w, router_b, expert_w, expert_b):
        import jax, jax.numpy as jnp
        import numpy as np
        B, S, D, E = (2, 512, 256, 8)
        logits = jnp.einsum('bsd,ed->bse', x, router_w) + router_b
        probs = jax.nn.softmax(logits, axis=-1)
        weights = jnp.max(probs, axis=-1)
        top1 = jnp.argmax(probs, axis=-1)
        y_all = jnp.einsum('bsd,eod->bseo', x, expert_w) + expert_b
        y = jnp.take_along_axis(y_all, top1[:, :, None, None], axis=2)[:, :, 0, :]
        out = y * weights[:, :, None]
        return out

    def _L1_xattn_ref(query, key, value, mask, Wq, bq, Wk, bk, Wv, bv, Wo, bo):
        import jax, jax.numpy as jnp
        import numpy as np
        H = 16
        D_MODEL = 256
        D_K = D_MODEL // H
        NEG = -1000000000.0

        def _split_heads(x, B, S):
            return x.reshape(B, S, H, D_K).transpose(0, 2, 1, 3)
        B, S, _ = query.shape
        q = _split_heads(query @ Wq.T + bq, B, S)
        k = _split_heads(key @ Wk.T + bk, B, S)
        v = _split_heads(value @ Wv.T + bv, B, S)
        scores = jnp.einsum('bhqd,bhkd->bhqk', q, k) / jnp.sqrt(jnp.float32(D_K))
        m = mask[:, None, :, :]
        scores = jnp.where(m == 0, jnp.float32(NEG), scores)
        p_attn = jax.nn.softmax(scores, axis=-1)
        x = jnp.einsum('bhqk,bhkd->bhqd', p_attn, v)
        x = x.transpose(0, 2, 1, 3).reshape(B, S, H * D_K)
        return x @ Wo.T + bo

    def _L1_ffn_ref(x, w_gate, w_up, w_down):
        import jax, jax.numpy as jnp
        import numpy as np
        HIDDEN = 256
        INNER = 1024

        def _weight_quant(w):
            scale = 1.0 / jnp.clip(jnp.mean(jnp.abs(w)), 1e-05)
            wq = jnp.clip(jnp.round(w * scale), -1.0, 1.0) / scale
            return w + jax.lax.stop_gradient(wq - w)

        def _act_quant(x):
            scale = 127.0 / jnp.clip(jnp.max(jnp.abs(x), axis=-1, keepdims=True), 1e-05)
            xq = jnp.clip(jnp.round(x * scale), -128.0, 127.0) / scale
            return x + jax.lax.stop_gradient(xq - x)

        def _bitlinear(x, w):
            return jnp.einsum('bsi,oi->bso', _act_quant(x), _weight_quant(w))
        gate = jax.nn.silu(_bitlinear(x, w_gate))
        up = _bitlinear(x, w_up)
        return _bitlinear(gate * up, w_down)
    x = x + _L0_xattn_ref(_layernorm(x, axis=-1), ctx_1024, ctx_1024, L0_xattn_Wq, L0_xattn_bq, L0_xattn_Wout, L0_xattn_bout)
    x = x + _L0_ffn_ref(_layernorm(x, axis=-1), L0_ffn_router_w, L0_ffn_router_b, L0_ffn_expert_w, L0_ffn_expert_b)
    x = x + _L1_xattn_ref(_layernorm(x, axis=-1), ctx_1024, ctx_1024, mask_Bx1xS2_ik0, L1_xattn_Wq, L1_xattn_bq, L1_xattn_Wk, L1_xattn_bk, L1_xattn_Wv, L1_xattn_bv, L1_xattn_Wo, L1_xattn_bo)
    x = x + _L1_ffn_ref(_layernorm(x, axis=-1), L1_ffn_w_gate, L1_ffn_w_up, L1_ffn_w_down)
    return x

_drawn_inputs = setup_inputs


def setup_inputs(seed=0):
    import zlib

    import numpy as np

    out = dict(_drawn_inputs(seed))
    spreads = {'L0_xattn_bq': (0.0, 0.1),
     'L0_xattn_bout': (0.0, 0.1),
     'L0_ffn_router_b': (0.0, 0.269),
     'L0_ffn_expert_b': (0.0, 0.435)}
    factors = {'L1_xattn_bq': 3.548, 'L1_xattn_bk': 8.0}
    for name, (base, spread) in spreads.items():
        noise = np.random.default_rng([zlib.crc32(name.encode()), seed]).standard_normal(out[name].shape)
        drawn = base * np.exp(spread * noise) if base else spread * noise
        out[name] = jnp.asarray(drawn.astype(out[name].dtype))
    for name, factor in factors.items():
        out[name] = (out[name] * factor).astype(out[name].dtype)
    return out
```

```python
from contextlib import ExitStack

import concourse.bass as bass
from concourse import mybir

F32 = mybir.dt.float32
F32R = mybir.dt.float32r
BF16 = mybir.dt.bfloat16
I32 = mybir.dt.int32
U32 = mybir.dt.uint32
ALU = mybir.AluOpType
ACT = mybir.ActivationFunctionType
AX_X = mybir.AxisListType.X

P = 128
NB, S, D = 32, 256, 256
T = S // P
KT = D // P
L0_HEADS = 16
L0_DH = D // L0_HEADS
K_TOP = 12
NE = 8
H = 16
DH = D // H
INNER = 1024
IC = INNER // P
GC = INNER // 256
LN_EPS = 1e-5
NEG = -3.0e38
MAGIC = 12582912.0
BIG_HI, BIG_LO = 1000079360.0, -79360.0
GROUP = 8
NG = NB // GROUP
ZW = 2 * P - L0_DH
SLOTS = 16
DEPTH = 74
PEEL, UNROLL = 8, 4
QROWS, AROWS = 96, 98


class Batch:

    def __init__(self, n, residue, group):
        self.n, self.residue, self.group = n, residue, group
        self.par = residue % 2
        self.quad = residue % 4

    def ago(self, k):
        return batch(self.residue - k, self.group)

    @property
    def exists(self):
        return not isinstance(self.n, int) or 0 <= self.n < NB

    def turn(self):
        if self.group is None:
            return self.residue // 2 + 1
        return self.group * 2 + (self.residue // 2 + 1)

    def fours(self, k):
        return 4 * self.n + k if self.group is None else self.group * 16 + (4 * self.residue + k)


def batch(residue, group):
    return Batch(residue if group is None else UNROLL * group + residue, residue, group)


def after(eng, sem, b):
    if b.exists:
        eng.wait_ge(sem, b.n + 1)


def after4(eng, sem, b, k):
    if b.exists:
        eng.wait_ge(sem, b.fours(k))


def landed(eng, sems, b, each):
    if b.exists:
        eng.wait_ge(sems[b.par], b.turn() * each)


def apart(eng, parted):
    eng.sem_inc(parted, 1)


def pipeline(eng, work):
    def step(residue, group):
        for s in range(SLOTS):
            for off in reversed(range(s, DEPTH, SLOTS)):
                b = batch(residue - off // SLOTS, group)
                if b.exists:
                    work(off, b)

    for i in range(PEEL):
        step(i, None)
    with eng.Fori(PEEL // UNROLL, NB // UNROLL) as g:
        for j in range(UNROLL):
            step(j, g)
    for i in range(NB, NB + (DEPTH - 1) // SLOTS):
        step(i, None)


def build(nc, x, ctxT, mask, wq0, bq0, wout_r, bout, rwT, rb, ewT, eb, wqT, bq, wkT, bk, wvT, bv,
          woT, bo, wgT, wuT, wdT, out):
    with ExitStack() as ctx:
        def sb(name, shape, dt=F32):
            return ctx.enter_context(nc.sbuf_tensor(name, shape, dt))

        def sem(name):
            return ctx.enter_context(nc.semaphore(name))

        def sems(name, n):
            return [sem(f"{name}{i}") for i in range(n)]

        def scratch(name, shape, dt=F32):
            return nc.dram_tensor(name, shape, dt, kind="Internal").ap()

        gram_d = scratch("gram_d", [S, 2 * S])
        lagw_d = scratch("lagw_d", [1, 2 * S])
        attn0_d = scratch("attn0_d", [NB * L0_DH, D])
        ksplit_d = scratch("ksplit_d", [2, 2, D, S])
        qsplit_d = scratch("qsplit_d", [2, 2, D, S])

        area_at = -(-nc.sbuf_base // 32) * 32
        area = sb("area", [P, 4 * H * S])
        qs = [nc.alloc_sbuf_tensor_at(f"qs{i}", [P, H, S], F32R, offset=area_at + 4 * H * S * i) for i in range(2)]
        ks = [nc.alloc_sbuf_tensor_at(f"ks{i}", [P, H, S], F32R, offset=area_at + 4 * H * S * (2 + i)) for i in range(2)]

        ident = sb("ident", [P, P])
        identb = sb("identb", [P, P], BF16)
        ones = sb("ones", [P, P])
        mhalf = sb("mhalf", [P, 2])
        iota8 = sb("iota8", [P, NE])
        big = sb("big", [2, 1])
        wk = sb("wk", [P, KT, D])
        wq = sb("wq", [P, KT, D])
        wv = sb("wv", [P, KT, D])
        wo = sb("wo", [P, KT, D])
        bk_c = sb("bk_c", [P, KT])
        bq_c = sb("bq_c", [P, KT])
        bq4 = sb("bq4", [P, KT])
        bv_r = sb("bv_r", [P, D])
        bo_r = sb("bo_r", [P, D])
        rb_r = sb("rb_r", [P, NE])
        eb_s = sb("eb_s", [NE, D])
        rwh = sb("rwh", [P, KT, P], F32R)
        rwl = sb("rwl", [P, KT, P], F32R)
        ewh = sb("ewh", [P, KT, NE * D], F32R)
        ewl = sb("ewl", [P, KT, NE * D], F32R)
        wg = sb("wg", [P, KT, INNER], BF16)
        wu = sb("wu", [P, KT, INNER], BF16)
        wd = sb("wd", [P, IC, D], BF16)
        wabs = sb("wabs", [P, 3])
        wmean = sb("wmean", [P, 3])
        wscale = sb("wscale", [P, 3])
        hgate = sb("hgate", [P, 1])

        xl = sb("xl", [P, 2, T, D])
        a0 = sb("a0", [P, 2, D])
        ct = sb("ct", [P, 2, KT, S])
        mk = sb("mk", [P, S], I32)
        m01 = sb("m01", [P, S])
        mbias = sb("mbias", [2, S], F32R)
        x2 = sb("x2", [P, T, D])
        x3 = sb("x3", [P, 4, T, D])
        xn = sb("xn", [P, T, D])
        xah = sb("xah", [P, KT, S], F32R)
        xal = sb("xal", [P, KT, S], F32R)
        xbt = sb("xbt", [P, KT, S])
        pf = sb("pf", [P, KT, S])
        ph = sb("ph", [P, KT, S], F32R)
        pl = sb("pl", [P, KT, S], F32R)
        va = sb("va", [P, 2, T, H * 32])
        pt = sb("pt", [P, 4, 2, S])
        ot = sb("ot", [P, 4, S])
        on = sb("on", [P, T, D])
        otn = sb("otn", [P, KT, S])
        xq_n = on
        xq = sb("xq", [P, T, D], BF16)
        xqt = sb("xqt", [P, KT, S], BF16)
        th = sb("th", [P, 256])
        t1 = sb("t1", [P, 256])
        hid = sb("hid", [P, T, INNER])
        hq = sb("hq", [P, INNER], BF16)
        hqt = sb("hqt", [P, IC, P], BF16)
        outt = sb("outt", [P, T, D])
        nmh = sb("nmh", [H, S], F32R)
        nml = sb("nml", [H, S], F32R)
        lt = sb("lt", [NE, S])
        gt = sb("gt", [NE, S])
        mx = sb("mx", [P, T, H])
        bn = sb("bn", [P, 3, T, 6])
        mv = sb("mv", [P, 3, T, 2])
        ve = sb("ve", [P, 3, T])
        rs = sb("rs", [P, 3, T])
        lg = sb("lg", [P, T, NE])
        top8 = sb("top8", [P, T, 8])
        idx8 = sb("idx8", [P, T, 8], U32)
        idxf = sb("idxf", [P, T])
        ntop = sb("ntop", [P, T])
        elg = sb("elg", [P, T, NE])
        esum = sb("esum", [P, T])
        rsum = sb("rsum", [P, T])
        gg = sb("gg", [P, T, NE])
        rc = sb("rc", [P, T, H])
        am = sb("am", [P, T])
        amc = sb("amc", [P, T])
        amr = sb("amr", [P, T])
        sc = sb("sc", [P, T])
        dq = sb("dq", [P, T])
        ts_ = sb("ts_", [P, T])
        hc = sb("hc", [P, T])
        hm = sb("hm", [P, T])
        hmc = sb("hmc", [P, T])
        hmr = sb("hmr", [P, T])
        hf = sb("hf", [P, T])
        dqh = sb("dqh", [P, T])


        def part(at, *shape):
            n = 1
            for k in shape:
                n *= k
            names = "abc"[:len(shape)]
            v = area[:, at:at + n]
            if len(shape) == 1:
                return v
            return v.rearrange(f"p ({' '.join(names)}) -> p {' '.join(names)}", **dict(zip(names, shape)))

        raw_w = [part(0, 2048), part(2048, 2048), part(4096, 2048)]
        raw_e = part(6144, KT, NE * D)
        raw_r = part(10240, KT, NE)
        q0t = part(10256, NG, S)
        k0t = part(11280, NG, S)
        gram2 = part(12304, T, 2 * S)
        lagged = part(13328, T, S)
        v0 = part(13840, T, NG * P)
        circ = part(14864, T, S)
        wout_s = part(15376, T, D)
        bq0_c = part(15888, 1)
        wq_raw = part(15904, KT, L0_DH)
        xa = x3
        ca = va
        z = hid[:, 1, 0:KT * ZW].rearrange("p (k w) -> p k w", k=KT)
        xna = pt[:, 0:2]
        xta = pt[:, 2:4]
        wmix = on
        out16 = ot
        bout_r = t1
        corr = hid[0:1, 0, 0:3 * S].rearrange("p (a s) -> p a s", a=3)
        c8 = part(15936, 4, 8)[0:1]

        def ca_at(i):
            return ca[:, i // 2, :, (i % 2) * 256:(i % 2) * 256 + 256]

        bank = [ctx.enter_context(nc.psum_tensor(f"bank{i}", [P, 512], F32)) for i in range(6)]
        maxb = ctx.enter_context(nc.psum_tensor("maxb", [P, T, 512], F32))
        ebank, misc, cbank, obank, dbank = bank[0:2], bank[2], bank[3], bank[4], bank[5]

        def halves(b):
            return b[:, :].rearrange("p (a c) -> p a c", a=2)

        consts = sem("consts")
        parted = {e: sem(f"parted_{e}") for e in ("pool", "dve", "pe", "sp")}
        early_ld, raw_ld, w_ld = sem("early_ld"), sem("raw_ld"), sem("w_ld")
        z_made = sem("z_made")
        xa_ld, ca_ld = sems("xa_ld", 4), sems("ca_ld", 4)
        a_stats, a_var, a_rstd = sem("a_stats"), sem("a_var"), sem("a_rstd")
        a_xn, a_xnT, a_xt, a_mm, a_grp = sem("a_xn"), sem("a_xnT"), sem("a_xt"), sem("a_mm"), sem("a_grp")
        lagstep = sem("lagstep")
        v_ready, v_made = sem("v_ready"), sem("v_made")
        lag_dma = sem("lag_dma")
        tern, wsum = sem("tern"), sem("wsum")
        wsplit = sem("wsplit")
        stacks_ready = sem("stacks_ready")

        x_ld, c_ld, m_ld = sems("x_ld", 2), sems("c_ld", 2), sem("m_ld")
        k_wr, q_wr, ks_ld = sems("k_wr", 2), sems("q_wr", 2), sems("ks_ld", 2)
        qs_ld, mx_ld, out_st = sems("qs_ld", 2), sems("mx_ld", 2), sem("out_st")
        x2_made = sem("x2_made")
        lna_st, lna_var, lna_rstd, xna_made, xna_T = (sem("lna_st"), sem("lna_var"), sem("lna_rstd"),
                                                      sem("xna_made"), sem("xna_T"))
        lnb_st, lnb_var, lnb_rstd, xnb_made, xnb_T = (sem("lnb_st"), sem("lnb_var"), sem("lnb_rstd"),
                                                      sem("xnb_made"), sem("xnb_T"))
        xah_made, xal_made = sem("xah_made"), sem("xal_made")
        rt_ready, lt_made, rtt_ready, rchain, relg, rchain2, gT_ready, gt_made, gb_ready = (
            sem("rt_ready"), sem("lt_made"), sem("rtt_ready"), sem("rchain"), sem("relg"), sem("rchain2"),
            sem("gT_ready"), sem("gt_made"), sem("gb_ready"))
        x3_init, e_ready, e_half, e_sum = sem("x3_init"), sems("e_ready", 2), sems("e_half", 2), sems("e_sum", 2)
        m01_made, mb_made, kp_ready, kf_made, kh_made, kl_made, vp_ready, va_made = (
            sem("m01_made"), sem("mb_made"), sem("kp_ready"), sem("kf_made"), sem("kh_made"), sem("kl_made"),
            sem("vp_ready"), sem("va_made"))
        xbt_made, qp_ready, qf_made, qh_made, ql_made, bo_added = (
            sem("xbt_made"), sem("qp_ready"), sem("qf_made"), sem("qh_made"), sem("ql_made"), sem("bo_added"))
        mx_ready, mx_made = sems("mx_ready", 2), sems("mx_made", 2)
        mxT_ready, nmh_made, nml_made = sem("mxT_ready"), sem("nmh_made"), sem("nml_made")
        sc_ready, ex_made, pv_done, ot_made = sems("sc_ready", 4), sems("ex_made", 4), sems("pv_done", 2), sem("ot_made")
        otT_ready, rc_made, on_made = sems("otT_ready", 2), sems("rc_made", 2), sems("on_made", 2)
        onT_ready, otn_made, op_ready, x4_made = sem("onT_ready"), sem("otn_made"), sem("op_ready"), sem("x4_made")
        lnc_st, lnc_var, lnc_rstd, lnc_made = sem("lnc_st"), sem("lnc_var"), sem("lnc_rstd"), sem("lnc_made")
        qchain, qchain2, xq_made, xqT_ready, xqt_made = (
            sem("qchain"), sem("qchain2"), sem("xq_made"), sem("xqT_ready"), sem("xqt_made"))
        gu_ready, th_made, t1_made, hid_made = sems("gu_ready", 2), sems("th_made", 2), sems("t1_made", 2), sems("hid_made", 2)
        hchain, hqa_made, hq_made, hqT_ready, hqt_made, dn_ready, out_made = (
            sems("hchain", 2), sems("hqa_made", 2), sems("hq_made", 2), sems("hqT_ready", 2),
            sems("hqt_made", 2), sems("dn_ready", 2), sems("out_made", 2))

        N_EARLY, N_RAW, N_W = 3, 5, 11
        (L_GRAM, L_GRAM2, L_CORR, L_ROW, L_TOP, L_CUT, L_NEXT, L_SENT, L_CUT2, L_SEL, L_NEGM, L_EXP,
         L_WSEL, L_SUM, L_REC, L_W, L_MIX, L_WMIX, L_OUT, L_OUT16) = range(1, 21)
        ATTN0_STORED = 16 * 7

        block = ctx.enter_context(nc.Block())

        def pipeline_may_start(eng):
            eng.wait_ge(lag_dma, ATTN0_STORED)
            eng.wait_ge(tern, 12)
            eng.wait_ge(wsplit, 5)
            eng.wait_ge(w_ld, 16 * N_W)

        @block.sync
        def _(sp):
            def early_loads(b, j):
                xv = x[bass.ds(b, 1)].rearrange("o (t p) d -> (o p) t d", p=P)
                cv = ctxT[bass.ds(b, 1)].rearrange("o (k p) s -> (o p) k s", p=P)
                sp.dma_start(xa[:, j], xv).then_inc(xa_ld[j], 16)
                sp.dma_start(ca_at(j), cv).then_inc(ca_ld[j], 16)

            sp.dma_start(bq0_c, bass.AP(bq0.tensor, 0, [[0, GROUP], [1, L0_DH], [1, 1]])).then_inc(early_ld, 16)
            sp.dma_start(wq_raw, wq0.rearrange("(k p) n -> p k n", p=P)).then_inc(early_ld, 16)
            sp.dma_start(wout_s, wout_r.rearrange("(k p) n -> p k n", p=P)).then_inc(early_ld, 16)
            for b in range(4):
                early_loads(b, b)
            for src, dst in ((wgT, raw_w[0]), (wuT, raw_w[1])):
                sp.dma_start(dst.rearrange("p (k n) -> p k n", k=KT), src.rearrange("(k p) n -> p k n", p=P)).then_inc(raw_ld, 16)
            sp.dma_start(raw_w[2].rearrange("p (k n) -> p k n", k=IC), wdT.rearrange("(k p) n -> p k n", p=P)).then_inc(raw_ld, 16)
            sp.dma_start(raw_e, ewT.rearrange("(k p) n -> p k n", p=P)).then_inc(raw_ld, 16)
            sp.dma_start(raw_r, rwT.rearrange("(k p) n -> p k n", p=P)).then_inc(raw_ld, 16)
            with sp.Fori(1, NB // 4) as g:
                for j in range(4):
                    sp.wait_ge(a_xn, 4 * g + (j - 3))
                    sp.wait_ge(a_mm, 4 * g + (j - 3))
                    early_loads(4 * g + j, j)
            for dst, src in ((wq, wqT), (wk, wkT), (wv, wvT), (wo, woT)):
                sp.dma_start(dst[:], src.rearrange("(k p) n -> p k n", p=P)).then_inc(w_ld, 16)
            for dst, src in ((bq_c, bq), (bk_c, bk)):
                sp.dma_start(dst[:], src).then_inc(w_ld, 16)
            for dst, src, n in ((bv_r, bv, D), (bo_r, bo, D), (rb_r, rb, NE)):
                sp.dma_start(dst[:], bass.AP(src.tensor, 0, [[0, P], [1, n]])).then_inc(w_ld, 16)
            sp.dma_start(eb_s[:], eb).then_inc(w_ld, 16)
            sp.dma_start(bout_r[:], bass.AP(bout.tensor, 0, [[0, P], [1, D]])).then_inc(w_ld, 16)

            sp.wait_ge(lagstep, L_GRAM2)
            sp.dma_start(gram_d.rearrange("(t p) m -> p t m", p=P), gram2).then_inc(lag_dma, 16)
            sp.wait_ge(lag_dma, 16)
            for t in range(T):
                sp.dma_start(lagged[:, t], bass.AP(gram_d.tensor, t * P * (2 * S + 1), [[2 * S + 1, P], [1, S]]))\
                    .then_inc(lag_dma, 16)
            sp.wait_ge(lagstep, L_W)
            for i in range(2):
                sp.dma_start(lagw_d[:, i * S:(i + 1) * S], corr[:, 2, :]).then_inc(lag_dma, 16)
            sp.wait_ge(lag_dma, 16 * 5)
            sp.dma_start(circ, bass.AP(lagw_d.tensor, 1, [[1, P], [P, T], [1, S]])).then_inc(lag_dma, 16)
            sp.wait_ge(lagstep, L_OUT16)
            sp.dma_start(attn0_d.rearrange("(g p) d -> p g d", p=P), out16[:]).then_inc(lag_dma, 16)
            pipeline_may_start(sp)

            def work(o, b):
                if o == 0:
                    after(sp, x2_made, b.ago(2))
                    sp.dma_start(xl[:, b.par], x[bass.ds(b.n, 1)].rearrange("o (t p) d -> (o p) t d", p=P))\
                        .then_inc(x_ld[b.par], 16)
                    rows = attn0_d.rearrange("(b r) d -> b r d", r=L0_DH)[bass.ds(b.n, 1)]
                    sp.dma_start(a0[:, b.par], bass.AP(rows.tensor, rows.offset, [[0, P // L0_DH], [D, L0_DH], [1, D]],
                                                       runtime_checks=rows.runtime_checks)).then_inc(x_ld[b.par], 16)
                    after(sp, vp_ready, b.ago(2))
                    sp.dma_start(ct[:, b.par], ctxT[bass.ds(b.n, 1)].rearrange("o (k p) s -> (o p) k s", p=P))\
                        .then_inc(c_ld[b.par], 16)
                    after(sp, m01_made, b.ago(1))
                    row = mask[bass.ds(b.n, 1)]
                    sp.dma_start(mk[:], bass.AP(row.tensor, row.offset, [[0, P], [1, S]],
                                                runtime_checks=row.runtime_checks)).then_inc(m_ld, 16)
                if o == 13:
                    after(sp, kl_made, b)
                    apart(sp, parted["sp"])
                    landed(sp, ks_ld, b.ago(2), 64)
                    for i, src in enumerate((ph, pl)):
                        sp.dma_start(ksplit_d[b.par, i].rearrange("(k p) s -> p k s", p=P), src[:].bitcast(F32)).then_inc(k_wr[b.par], 16)
                if o == 21:
                    landed(sp, k_wr, b, 32)
                    apart(sp, parted["sp"])
                    after4(sp, sc_ready[3], b.ago(2), 4)
                    if b.residue < 2 and b.group is None:
                        sp.wait_ge(stacks_ready, 7)
                    for row, i in ((0, 0), (DH, 0), (2 * DH, 1)):
                        sp.dma_start(ks[b.par][row:row + DH].bitcast(F32), ksplit_d[b.par, i].rearrange("(h d) s -> d h s", d=DH))\
                            .then_inc(ks_ld[b.par], 16)
                    after(sp, mb_made, b)
                    sp.dma_start(ks[b.par][3 * DH:3 * DH + 2].bitcast(F32), mbias[:].bitcast(F32).unsqueeze(1).to_broadcast([2, H, S]))\
                        .then_inc(ks_ld[b.par], 16)
                if o == 22:
                    after(sp, ql_made, b)
                    apart(sp, parted["sp"])
                    landed(sp, qs_ld, b.ago(2), 48)
                    for i, src in enumerate((ph, pl)):
                        sp.dma_start(qsplit_d[b.par, i].rearrange("(k p) s -> p k s", p=P), src[:].bitcast(F32)).then_inc(q_wr[b.par], 16)
                if o == 23:
                    landed(sp, q_wr, b, 32)
                    apart(sp, parted["sp"])
                    after4(sp, sc_ready[3], b.ago(2), 4)
                    for row, i in ((0, 0), (DH, 1), (2 * DH, 0)):
                        sp.dma_start(qs[b.par][row:row + DH].bitcast(F32), qsplit_d[b.par, i].rearrange("(h d) s -> d h s", d=DH))\
                            .then_inc(qs_ld[b.par], 16)
                if o == 35:
                    after(sp, nml_made, b)
                    for i, src in enumerate((nmh, nml)):
                        sp.dma_start(qs[b.par][QROWS + i:QROWS + i + 1].bitcast(F32), src[:].bitcast(F32)).then_inc(mx_ld[b.par], 16)
                if o == 73:
                    after(sp, out_made[1], b)
                    sp.dma_start(out[bass.ds(b.n, 1)].rearrange("o (t p) d -> (o p) t d", p=P), outt[:]).then_inc(out_st, 16)

            pipeline(sp, work)
            sp.wait_ge(out_st, 16 * NB)

        @block.gpsimd
        def _(pool):
            pool.memset(ident[:], 0.0).then_inc(consts, 1)
            pool.memset(ones[:], 1.0).then_inc(consts, 1)
            pool.memset(mhalf[:], -0.5).then_inc(consts, 1)
            pool.memset(z, 0.0).then_inc(consts, 1)
            for e in range(NE):
                pool.memset(iota8[:, e:e + 1], float(e))
            pool.memset(big[0:2, :], BIG_LO).then_inc(consts, 1)
            pool.wait_ge(consts, 5)
            pool.memset(big[0:1, :], BIG_HI).then_inc(consts, 1)
            pool.affine_select(out=ident[:], in_=ident[:], compare_op=ALU.not_equal, fill=1.0, base=0,
                               pattern=[[-1, P]], channel_multiplier=1).then_inc(consts, 1)
            pool.wait_ge(consts, 7)
            pool.tensor_copy(identb[:], ident[:]).then_inc(consts, 1)

            def rstd(b, j):
                pool.wait_ge(a_var, b + 1)
                pool.tensor_tensor(rs[:, j], ve[:, j], mhalf[:], ALU.pow).then_inc(a_rstd, 1)

            for b in range(2):
                rstd(b, b % 2)
            with pool.Fori(1, NB // 2) as g:
                for j in range(2):
                    rstd(2 * g + j, j)

            pool.wait_ge(raw_ld, 16 * N_RAW)
            pool.tensor_scalar(ewh[:], raw_e, 1.0, None, ALU.mult).then_inc(wsplit, 1)
            pool.memset(rwh[:].bitcast(F32), 0.0)
            pool.memset(rwl[:].bitcast(F32), 0.0).then_inc(wsplit, 1)
            pool.wait_ge(wsplit, 2)
            pool.tensor_scalar(rwh[:, :, 0:NE], raw_r, 1.0, None, ALU.mult).then_inc(wsplit, 1)
            pool.tensor_tensor(ewl[:], raw_e, ewh[:].bitcast(F32), ALU.subtract).then_inc(wsplit, 1)
            pool.wait_ge(wsplit, 4)
            pool.tensor_tensor(rwl[:, :, 0:NE], raw_r, rwh[:, :, 0:NE].bitcast(F32), ALU.subtract).then_inc(wsplit, 1)
            pipeline_may_start(pool)

            def stacks():
                pool.memset(va[:], 1.0).then_inc(stacks_ready, 1)
                for i in range(2):
                    pool.memset(qs[i][:].bitcast(F32), 0.0).then_inc(stacks_ready, 1)
                    pool.memset(ks[i][:].bitcast(F32), 0.0).then_inc(stacks_ready, 1)
                pool.wait_ge(stacks_ready, 5)
                for i in range(2):
                    pool.memset(ks[i][QROWS:P].bitcast(F32), 1.0)
                    pool.memset(qs[i][32:64].bitcast(F32), 1.0).then_inc(stacks_ready, 1)
                pool.wait_ge(stacks_ready, 7)

            def normalise(i, src, b, st, made, rstd_made):
                pool.tensor_tensor(rs[:, i], ve[:, i], mhalf[:], ALU.pow).then_inc(rstd_made, 1)
                after(pool, rstd_made, b)
                apart(pool, parted["pool"])
                for t in range(T):
                    ins = pool.tensor_scalar(xn[:, t], src[:, t], mv[:, i, t, 0:1], rs[:, i, t:t + 1],
                                             ALU.subtract, ALU.mult)
                ins.then_inc(made, 1)

            def work(o, b):
                if o == 2:
                    landed(pool, x_ld, b, 32)
                    after(pool, x3_init, b.ago(1))
                    pool.tensor_tensor(x2[:], xl[:, b.par], a0[:, b.par].unsqueeze(1).to_broadcast([P, T, D]),
                                       ALU.add).then_inc(x2_made, 1)
                if o == 4:
                    after(pool, lna_var, b)
                    after(pool, xnb_T, b.ago(1))
                    normalise(0, x2, b, lna_st, xna_made, lna_rstd)
                    if b.group is None and b.residue == 0:
                        stacks()
                if o == 12:
                    after(pool, kf_made, b)
                    landed(pool, q_wr, b.ago(1), 32)
                    apart(pool, parted["pool"])
                    pool.tensor_scalar(ph[:], pf[:], 1.0, None, ALU.mult).then_inc(kh_made, 1)
                    after(pool, kh_made, b)
                    pool.tensor_tensor(pl[:], pf[:], ph[:].bitcast(F32), ALU.subtract).then_inc(kl_made, 1)
                if o == 19:
                    after(pool, lnb_var, b)
                    after(pool, xna_T, b)
                    normalise(1, x3[:, b.quad], b, lnb_st, xnb_made, lnb_rstd)
                if o == 20:
                    after(pool, xnb_made, b)
                    pool.tensor_tensor(x3[:, b.quad], x3[:, b.quad], bo_r[:].unsqueeze(1).to_broadcast([P, T, D]),
                                       ALU.add).then_inc(bo_added, 1)
                if o == 22:
                    after(pool, qf_made, b)
                    landed(pool, k_wr, b, 32)
                    apart(pool, parted["pool"])
                    pool.tensor_scalar(ph[:], pf[:], 1.0, None, ALU.mult).then_inc(qh_made, 1)
                    after(pool, qh_made, b)
                    pool.tensor_tensor(pl[:], pf[:], ph[:].bitcast(F32), ALU.subtract).then_inc(ql_made, 1)
                if o == 59:
                    after(pool, lnc_var, b)
                    pool.tensor_tensor(rs[:, 2], ve[:, 2], mhalf[:], ALU.pow).then_inc(lnc_rstd, 1)
                if o in (66, 70):
                    t = (o - 66) // 4
                    after(pool, hqa_made[t], b)
                    after(pool, hqT_ready[1 - t], b if t else b.ago(1))
                    apart(pool, parted["pool"])
                    pool.tensor_scalar(hq[:], hid[:, t], MAGIC, 127.0, ALU.subtract, ALU.min).then_inc(hq_made[t], 1)

            pipeline(pool, work)

        @block.scalar
        def _(act):
            act.wait_ge(early_ld, 16 * N_EARLY)

            def evacuate(b, j):
                act.wait_ge(a_xnT, b + 1)
                if not (isinstance(b, int) and b < 2):
                    act.wait_ge(a_mm, b - 1)
                act.activation(xta[:, j % 2], halves(bank[j % 2]), ACT.Copy).then_inc(a_xt, 1)

            def group_out(g, n):
                act.wait_ge(a_mm, n)
                act.activation(q0t[:, g], bank[2][:, 0:S], ACT.Identity, bias=bq0_c)
                act.activation(k0t[:, g], bank[3][:, 0:S], ACT.Identity, bias=bq0_c).then_inc(a_grp, 1)

            for b in range(GROUP):
                evacuate(b, b)
            with act.Fori(1, NG) as g:
                evacuate(GROUP * g, 0)
                act.wait_ge(a_mm, GROUP * g)
                act.activation(q0t.rearrange("p g s -> p (g s)")[:, bass.ds(g * S - S, S)], bank[2][:, 0:S],
                               ACT.Identity, bias=bq0_c)
                act.activation(k0t.rearrange("p g s -> p (g s)")[:, bass.ds(g * S - S, S)], bank[3][:, 0:S],
                               ACT.Identity, bias=bq0_c).then_inc(a_grp, 1)
                for j in range(1, GROUP):
                    evacuate(GROUP * g + j, j)
            group_out(NG - 1, NB)

            act.wait_ge(lagstep, L_GRAM)
            for t in range(T):
                act.activation(gram2[:, t, 0:S], bank[t][:, 0:S], ACT.Copy)
                ins = act.activation(gram2[:, t, S:2 * S], bank[t][:, 0:S], ACT.Copy)
            ins.then_inc(lagstep, 1)
            act.wait_ge(v_ready, 1)
            act.activation(v0[:, 0], bank[4][:, :], ACT.Copy)
            act.activation(v0[:, 1], maxb[:, 0], ACT.Copy).then_inc(v_made, 1)
            act.wait_ge(lagstep, L_NEGM)
            act.activation(corr[:, 2, :], corr[:, 0, :], ACT.Exp, bias=c8[:, 3, 0:1]).then_inc(lagstep, 1)
            act.wait_ge(lagstep, L_MIX)
            for t in range(T):
                ins = act.activation(wmix[:, t], bank[t][:, 0:D], ACT.Copy)
            ins.then_inc(lagstep, 1)
            pipeline_may_start(act)

            def work(o, b):
                if o == 5:
                    after(act, xna_T, b)
                    after4(act, e_ready[1], b.ago(1), 4)
                    act.activation(xah[:], halves(misc), ACT.Copy).then_inc(xah_made, 1)
                if o == 6:
                    after(act, rt_ready, b)
                    after(act, rtt_ready, b.ago(1))
                    act.activation(lt[:], misc[0:NE, 0:S], ACT.Copy).then_inc(lt_made, 1)
                if o == 7:
                    after4(act, rchain, b, 3)
                    after4(act, rchain2, b.ago(1), 4)
                    for t in range(T):
                        ins = act.activation(elg[:, t], lg[:, t], ACT.Exp, bias=ntop[:, t:t + 1],
                                             accum_out=esum[:, t:t + 1])
                    ins.then_inc(relg, 1)
                if o == 9:
                    after(act, gT_ready, b)
                    after(act, gb_ready, b.ago(1))
                    act.activation(gt[:], misc[0:NE, 0:S], ACT.Copy).then_inc(gt_made, 1)
                if o == 20:
                    after(act, xnb_T, b)
                    after(act, qp_ready, b.ago(1))
                    act.activation(xbt[:], halves(misc), ACT.Copy).then_inc(xbt_made, 1)
                if o == 21:
                    after(act, qp_ready, b)
                    after(act, kl_made, b)
                    for m in range(KT):
                        ins = act.activation(pf[:, m], misc[:, m * S:(m + 1) * S], ACT.Identity,
                                             bias=bq4[:, m:m + 1], scale=0.25)
                    ins.then_inc(qf_made, 1)
                if o == 34:
                    after(act, mxT_ready, b)
                    landed(act, mx_ld, b.ago(1), 32)
                    act.activation(nmh[:], misc[0:H, 0:S], ACT.Copy, scale=-1.0).then_inc(nmh_made, 1)
                if 37 <= o < 53:
                    s = o - 37
                    after4(act, sc_ready[s % 4], b, s // 4 + 1)
                    u = s // 2 - 2
                    if u >= 0:
                        after4(act, pv_done[u % 2], b, u // 2 + 1)
                    else:
                        after4(act, pv_done[u % 2], b.ago(1), (u + 8) // 2 + 1)
                    act.activation(pt[:, s % 4].rearrange("p a c -> p (a c)"), cbank[:, :], ACT.Exp).then_inc(ex_made[s % 4], 1)
                if 42 <= o < 58 and (o - 42) % 4 == 0:
                    g = (o - 42) // 4
                    after4(act, pv_done[1], b, g + 1)
                    if g == 0:
                        after(act, otT_ready[1], b.ago(1))
                    act.activation(ot[:, g], obank[:, 0:S], ACT.Copy).then_inc(ot_made, 1)
                if o == 57:
                    after(act, onT_ready, b)
                    after(act, op_ready, b.ago(1))
                    act.activation(otn[:], halves(dbank), ACT.Copy).then_inc(otn_made, 1)
                if o == 60:
                    after(act, xqT_ready, b)
                    after4(act, gu_ready[1], b.ago(1), 4)
                    act.activation(xqt[:].rearrange("p k s -> p (k s)"), dbank[:, 0:S].bitcast(BF16), ACT.Copy)\
                        .then_inc(xqt_made, 1)
                if 61 <= o < 69:
                    c = o - 61
                    after4(act, gu_ready[c % 2], b, c // 2 + 1)
                    if c:
                        after4(act, t1_made[(c - 1) % 2], b, (c - 1) // 2 + 1)
                    else:
                        after4(act, t1_made[1], b.ago(1), 4)
                    after4(act, qchain2, b, 2)
                    act.activation(th[:], dbank[:, 0:256], ACT.Tanh, scale=ts_[:, c // 4:c // 4 + 1])\
                        .then_inc(th_made[c % 2], 1)
                if o in (67, 71):
                    t = (o - 67) // 4
                    after(act, hqT_ready[t], b)
                    after(act, dn_ready[1 - t], b if t else b.ago(1))
                    act.activation(hqt[:].rearrange("p k s -> p (k s)"), dbank[:, :].bitcast(BF16), ACT.Copy)\
                        .then_inc(hqt_made[t], 1)

            pipeline(act, work)

        @block.vector
        def _(dve):
            def stats(src, i, st, var, b, n):
                for t in range(T):
                    dve.bn_stats(bn[:, i, t], src[:, t]).then_inc(st, 1)
                for t in range(T):
                    dve.wait_ge(st, n(t + 1))
                    apart(dve, parted["dve"])
                    dve.bn_aggr(mv[:, i, t], bn[:, i, t]).then_inc(st, 1)
                dve.wait_ge(st, n(4))
                dve.tensor_scalar(ve[:, i], mv[:, i, :, 1], LN_EPS, None, ALU.add).then_inc(var, 1)

            dve.wait_ge(consts, 8)
            dve.wait_ge(early_ld, 16 * N_EARLY)
            dve.tensor_copy(z[:, :, P - L0_DH:P], wq_raw).then_inc(z_made, 1)

            def early(b, j, turn, first):
                if first and j < 2:
                    pass
                else:
                    dve.wait_ge(a_xn, b - 1)
                    dve.wait_ge(a_rstd, b - 1)
                dve.wait_ge(xa_ld[j % 4], 16 * turn)
                stats(xa[:, j % 4], j % 2, a_stats, a_var, b, lambda k: 4 * b + k)

            def apply(b, j, first):
                dve.wait_ge(a_rstd, b + 1)
                if not (first and j < 2):
                    dve.wait_ge(a_xnT, b - 1)
                for t in range(T):
                    ins = dve.tensor_scalar(xna[:, j % 2, t], xa[:, j % 4, t], mv[:, j % 2, t, 0:1],
                                            rs[:, j % 2, t:t + 1], ALU.subtract, ALU.mult)
                ins.then_inc(a_xn, 1)

            for b in range(4):
                early(b, b, 1, True)
                if b:
                    apply(b - 1, b - 1, True)
            with dve.Fori(1, NB // 4) as g:
                for j in range(4):
                    early(4 * g + j, j, g + 1, False)
                    apply(4 * g + (j - 1), (j - 1) % 4, False)
            apply(NB - 1, 3, False)

            dve.wait_ge(raw_ld, 16 * N_RAW)
            for i in range(3):
                ins = dve.tensor_reduce(wabs[:, i:i + 1], raw_w[i], AX_X, ALU.add, apply_absolute_value=True)
            ins.then_inc(tern, 1)
            dve.wait_ge(wsum, 1)
            dve.tensor_scalar(wmean[:], bank[5][:, 0:3], 1.0 / (D * INNER), 1e-5, ALU.mult, ALU.max).then_inc(tern, 1)
            dve.wait_ge(tern, 2)
            dve.tensor_scalar(hgate[:], wmean[:, 0:1], 0.5, None, ALU.mult)
            dve.reciprocal(wscale[:], wmean[:]).then_inc(tern, 1)
            dve.wait_ge(tern, 3)
            for i in range(3):
                dve.tensor_scalar(raw_w[i], raw_w[i], wscale[:, i:i + 1], -1.0, ALU.mult, ALU.max).then_inc(tern, 1)

            dve.wait_ge(lagstep, L_CORR)
            dve.tensor_scalar(corr[:, 0, :], bank[2][0:1, 0:S], 1.0 / (NB * L0_DH), None, ALU.mult).then_inc(lagstep, 1)
            dve.wait_ge(lagstep, L_ROW)
            dve.max(c8[:, 0, :], corr[:, 0, :]).then_inc(lagstep, 1)
            dve.wait_ge(lagstep, L_TOP)
            dve.match_replace(corr[:, 1, :], c8[:, 0, :], corr[:, 0, :], NEG).then_inc(lagstep, 1)
            dve.wait_ge(lagstep, L_CUT)
            dve.max(c8[:, 1, :], corr[:, 1, :]).then_inc(lagstep, 1)
            dve.wait_ge(lagstep, L_NEXT)
            dve.memset(c8[:, 1, K_TOP - 8:8], NEG).then_inc(lagstep, 1)
            dve.wait_ge(lagstep, L_SENT)
            dve.match_replace(corr[:, 1, :], c8[:, 1, :], corr[:, 1, :], NEG).then_inc(lagstep, 1)
            dve.wait_ge(lagstep, L_CUT2)
            dve.tensor_scalar(corr[:, 1, :], corr[:, 1, :], NEG, None, ALU.is_equal).then_inc(lagstep, 1)
            dve.wait_ge(lagstep, L_SEL)
            dve.tensor_scalar(c8[:, 3, 0:1], c8[:, 0, 0:1], -1.0, None, ALU.mult).then_inc(lagstep, 1)
            dve.wait_ge(lagstep, L_EXP)
            dve.tensor_tensor(corr[:, 2, :], corr[:, 2, :], corr[:, 1, :], ALU.mult).then_inc(lagstep, 1)
            dve.wait_ge(lagstep, L_WSEL)
            dve.tensor_reduce(c8[:, 2, 0:1], corr[:, 2, :], AX_X, ALU.add).then_inc(lagstep, 1)
            dve.wait_ge(lagstep, L_SUM)
            dve.reciprocal(c8[:, 2, 1:2], c8[:, 2, 0:1]).then_inc(lagstep, 1)
            dve.wait_ge(lagstep, L_REC)
            dve.tensor_scalar(corr[:, 2, :], corr[:, 2, :], c8[:, 2, 1:2], None, ALU.mult).then_inc(lagstep, 1)

            for i in range(3):
                dve.wait_ge(tern, 4 + i)
                dve.tensor_scalar(raw_w[i], raw_w[i], 1.0, MAGIC, ALU.min, ALU.add).then_inc(tern, 1)
            dve.wait_ge(w_ld, 16 * N_W)
            dve.tensor_scalar(bq4[:], bq_c[:], 0.25, None, ALU.mult)
            for i, w in enumerate((wg, wu, wd)):
                dve.wait_ge(tern, 7 + i)
                dve.tensor_scalar(w[:].rearrange("p k n -> p (k n)"), raw_w[i], MAGIC, None, ALU.subtract).then_inc(tern, 1)
            dve.wait_ge(lagstep, L_OUT)
            for g in range(NG):
                b_ = bank[g // 2][:, (g % 2) * D:(g % 2) * D + D]
                ins = dve.tensor_tensor(out16[:, g], b_, bout_r[:], ALU.add)
            ins.then_inc(lagstep, 1)
            pipeline_may_start(dve)

            def work(o, b):
                if o == 3:
                    after(dve, x2_made, b)
                    after(dve, xna_made, b.ago(1))
                    stats(x2, 0, lna_st, lna_var, b, b.fours)
                if o == 5:
                    after(dve, xah_made, b)
                    dve.tensor_tensor(xal[:], halves(misc), xah[:].bitcast(F32), ALU.subtract).then_inc(xal_made, 1)
                    dve.wait_ge(m_ld, b.n * 16 + 16)
                    after(dve, kf_made, b.ago(1))
                    dve.tensor_scalar(m01[:], mk[:], 0, None, ALU.not_equal).then_inc(m01_made, 1)
                if o == 12:
                    after(dve, m01_made, b)
                    landed(dve, ks_ld, b.ago(1), 64)
                    dve.tensor_scalar(mbias[:], m01[0:2], 1.0, big[:, 0:1], ALU.subtract, ALU.mult).then_inc(mb_made, 1)
                if o == 7:
                    after(dve, rtt_ready, b)
                    after(dve, relg, b.ago(1))
                    dve.tensor_tensor(lg[:], misc[:, 0:T * NE].rearrange("p (t e) -> p t e", e=NE),
                                      rb_r[:].unsqueeze(1).to_broadcast([P, T, NE]), ALU.add).then_inc(rchain, 1)
                    after4(dve, rchain, b, 1)
                    apart(dve, parted["dve"])
                    for t in range(T):
                        ins = dve.max(top8[:, t], lg[:, t])
                    ins.then_inc(rchain, 1)
                    after4(dve, rchain, b, 2)
                    dve.tensor_scalar(ntop[:], top8[:, :, 0], -1.0, None, ALU.mult).then_inc(rchain, 1)
                    apart(dve, parted["dve"])
                    for t in range(T):
                        ins = dve.max_index(idx8[:, t], top8[:, t], lg[:, t])
                    ins.then_inc(rchain, 1)
                    after4(dve, rchain, b, 4)
                    dve.tensor_copy(idxf[:], idx8[:, :, 0]).then_inc(rchain2, 1)
                if o == 8:
                    after(dve, relg, b)
                    dve.reciprocal(rsum[:], esum[:]).then_inc(rchain2, 1)
                    after4(dve, rchain2, b, 2)
                    after(dve, gT_ready, b.ago(1))
                    after4(dve, e_sum[1], b.ago(1), 4)
                    for t in range(T):
                        dve.tensor_scalar(gg[:, t], iota8[:], idxf[:, t:t + 1], rsum[:, t:t + 1],
                                          ALU.is_equal, ALU.mult).then_inc(rchain2, 1)
                if o == 10:
                    after(dve, gb_ready, b)
                    after(dve, out_made[1], b.ago(4))
                    dve.tensor_tensor(x3[:, b.quad], halves(misc), x2[:], ALU.add).then_inc(x3_init, 1)
                if 10 <= o < 18:
                    t, p = (o - 10) % 2, (o - 10) // 2
                    after4(dve, e_ready[t], b, p + 1)
                    for j in range(2):
                        if p == 0 and j == 0:
                            after(dve, x3_init, b)
                        elif j == 0:
                            after4(dve, e_sum[t], b, p)
                        else:
                            after4(dve, e_half[t], b, p + 1)
                        dve.scalar_tensor_tensor(out=x3[:, b.quad, t], in0=ebank[t][:, j * D:(j + 1) * D],
                                                 scalar=gg[:, t, 2 * p + j:2 * p + j + 1], in1=x3[:, b.quad, t],
                                                 op0=ALU.mult, op1=ALU.add).then_inc((e_half, e_sum)[j][t], 1)
                if o == 11:
                    after(dve, kp_ready, b)
                    after(dve, ql_made, b.ago(1))
                    for m in range(KT):
                        ins = dve.scalar_tensor_tensor(out=pf[:, m], in0=misc[:, m * S:(m + 1) * S],
                                                       scalar=bk_c[:, m:m + 1], in1=m01[:], op0=ALU.add, op1=ALU.mult)
                    ins.then_inc(kf_made, 1)
                if o == 18:
                    for t in range(T):
                        after4(dve, e_sum[t], b, 4)
                    after(dve, xnb_made, b.ago(1))
                    stats(x3[:, b.quad], 1, lnb_st, lnb_var, b, b.fours)
                if o == 22:
                    after(dve, vp_ready, b)
                    after4(dve, pv_done[1], b.ago(2), 4)
                    if b.group is None and b.residue < 2:
                        dve.wait_ge(stacks_ready, 7)
                    v = va[:, b.par].rearrange("p t (h c) -> p t h c", c=32)
                    for t in range(T):
                        ins = dve.tensor_tensor(v[:, t, :, 0:DH], misc[:, t * D:(t + 1) * D].rearrange("p (h c) -> p h c", c=DH),
                                                bv_r[:].rearrange("p (h c) -> p h c", c=DH), ALU.add)
                    ins.then_inc(va_made, 1)
                if 26 <= o < 34:
                    p = o - 26
                    after4(dve, mx_ready[p % 2], b, p // 2 + 1)
                    if p == 0:
                        after(dve, mxT_ready, b.ago(1))
                    dve.tensor_reduce(mx[:, :, 2 * p:2 * p + 2], maxb[:].rearrange("p t (h s) -> p t h s", h=2),
                                      AX_X, ALU.max).then_inc(mx_made[p % 2], 1)
                if o == 34:
                    after(dve, nmh_made, b)
                    dve.scalar_tensor_tensor(out=nml[:], in0=misc[0:H, 0:S], scalar=-1.0, in1=nmh[:].bitcast(F32),
                                             op0=ALU.mult, op1=ALU.subtract).then_inc(nml_made, 1)
                if o in (55, 56):
                    t = o - 55
                    after(dve, otT_ready[t], b)
                    v = dbank[:].rearrange("p (h c) -> p h c", c=32)
                    if t == 0:
                        after(dve, on_made[1], b.ago(1))
                    dve.reciprocal(rc[:, t], v[:, :, DH]).then_inc(rc_made[t], 1)
                    after(dve, rc_made[t], b)
                    after(dve, onT_ready, b.ago(1))
                    dve.tensor_tensor(on[:, t].rearrange("p (h c) -> p h c", c=DH), v[:, :, 0:DH],
                                      rc[:, t].unsqueeze(2).to_broadcast([P, H, DH]), ALU.mult).then_inc(on_made[t], 1)
                if o == 58:
                    after(dve, op_ready, b)
                    after(dve, bo_added, b)
                    dve.tensor_tensor(x3[:, b.quad], halves(dbank), x3[:, b.quad], ALU.add).then_inc(x4_made, 1)
                    after(dve, x4_made, b)
                    stats(x3[:, b.quad], 2, lnc_st, lnc_var, b, b.fours)
                if o == 59:
                    x4 = x3[:, b.quad]
                    after(dve, lnc_rstd, b)
                    for t in range(T):
                        ins = dve.tensor_scalar(xq_n[:, t], x4[:, t], mv[:, 2, t, 0:1], rs[:, 2, t:t + 1],
                                                ALU.subtract, ALU.mult)
                    ins.then_inc(lnc_made, 1)
                    after(dve, lnc_made, b)
                    dve.tensor_reduce(am[:], xq_n[:], AX_X, ALU.max, apply_absolute_value=True).then_inc(qchain, 1)
                    after4(dve, qchain, b, 1)
                    dve.tensor_scalar(amc[:], am[:], 1e-5, None, ALU.max).then_inc(qchain, 1)
                    after4(dve, qchain, b, 2)
                    dve.reciprocal(amr[:], amc[:]).then_inc(qchain, 1)
                    dve.tensor_scalar(dq[:], amc[:], 1.0 / 127.0, None, ALU.mult).then_inc(qchain2, 1)
                    after4(dve, qchain, b, 3)
                    dve.tensor_scalar(sc[:], amr[:], 127.0, None, ALU.mult).then_inc(qchain, 1)
                    after4(dve, qchain2, b, 1)
                    after4(dve, th_made[1], b.ago(1), 4)
                    dve.tensor_scalar(ts_[:], dq[:], hgate[:, 0:1], None, ALU.mult).then_inc(qchain2, 1)
                    after4(dve, qchain, b, 4)
                    dve.tensor_scalar(xq_n[:, 0], xq_n[:, 0], sc[:, 0:1], MAGIC, ALU.mult, ALU.add)
                    after4(dve, qchain2, b, 2)
                    dve.scalar_tensor_tensor(out=hc[:], in0=ts_[:], scalar=wmean[:, 1:2], in1=dq[:],
                                             op0=ALU.mult, op1=ALU.mult).then_inc(qchain2, 1)
                    dve.tensor_scalar(xq_n[:, 1], xq_n[:, 1], sc[:, 1:2], MAGIC, ALU.mult, ALU.add).then_inc(qchain2, 1)
                    after4(dve, qchain2, b, 4)
                    after(dve, xqT_ready, b.ago(1))
                    dve.tensor_scalar(xq[:], xq_n[:], MAGIC, 127.0, ALU.subtract, ALU.min).then_inc(xq_made, 1)
                if 61 <= o < 69:
                    c = o - 61
                    after4(dve, th_made[c % 2], b, c // 2 + 1)
                    if c:
                        after4(dve, hid_made[(c - 1) % 2], b, (c - 1) // 2 + 1)
                    else:
                        after4(dve, hid_made[1], b.ago(1), 4)
                    dve.scalar_tensor_tensor(out=t1[:], in0=th[:], scalar=1.0, in1=dbank[:, 0:256],
                                             op0=ALU.add, op1=ALU.mult).then_inc(t1_made[c % 2], 1)
                    after4(dve, t1_made[c % 2], b, c // 2 + 1)
                    if c % 4 == 0:
                        after(dve, hq_made[c // 4], b.ago(1))
                    dve.tensor_tensor(hid[:, c // 4, (c % 4) * 256:(c % 4) * 256 + 256], dbank[:, 256:512], t1[:],
                                      ALU.mult).then_inc(hid_made[c % 2], 1)
                if o in (65, 69):
                    t = (o - 65) // 4
                    for i in range(2):
                        after4(dve, hid_made[i], b, 2 * (t + 1))
                    dve.tensor_reduce(hm[:, t:t + 1], hid[:, t], AX_X, ALU.max, apply_absolute_value=True).then_inc(hchain[t], 1)
                    after4(dve, hchain[t], b, 1)
                    dve.tensor_scalar(hmc[:, t:t + 1], hm[:, t:t + 1], hc[:, t:t + 1], 1e-5, ALU.mult, ALU.max).then_inc(hchain[t], 1)
                    after4(dve, hchain[t], b, 2)
                    dve.reciprocal(hmr[:, t:t + 1], hmc[:, t:t + 1]).then_inc(hchain[t], 1)
                    after4(dve, hchain[t], b, 3)
                    dve.scalar_tensor_tensor(out=hf[:, t:t + 1], in0=hmr[:, t:t + 1], scalar=127.0, in1=hc[:, t:t + 1],
                                             op0=ALU.mult, op1=ALU.mult).then_inc(hchain[t], 1)
                    after4(dve, hchain[t], b, 4)
                    dve.tensor_scalar(hid[:, t], hid[:, t], hf[:, t:t + 1], MAGIC, ALU.mult, ALU.add)
                    dve.tensor_scalar(dqh[:, t:t + 1], hmc[:, t:t + 1], 1.0 / 127.0, wmean[:, 2:3], ALU.mult, ALU.mult)\
                        .then_inc(hqa_made[t], 1)
                if o in (68, 72):
                    t = (o - 68) // 4
                    after(dve, dn_ready[t], b)
                    after(dve, hqa_made[t], b)
                    if t == 0 and b.ago(1).exists:
                        dve.wait_ge(out_st, b.n * 16)
                    dve.scalar_tensor_tensor(out=outt[:, t], in0=dbank[:, 0:D], scalar=dqh[:, t:t + 1],
                                             in1=x3[:, b.quad, t], op0=ALU.mult, op1=ALU.add).then_inc(out_made[t], 1)

            pipeline(dve, work)

        @block.tensor
        def _(pe):
            pe.wait_ge(consts, 8)
            pe.wait_ge(z_made, 1)

            def transposes(b, j, first):
                pe.wait_ge(a_xn, b + 1)
                if not (first and j < 2):
                    pe.wait_ge(a_xt, b - 1)
                for k in range(KT):
                    for t in range(T):
                        ins = pe.transpose(bank[j % 2][:, k * S + t * P:k * S + (t + 1) * P],
                                           xna[:, j % 2, t, k * P:(k + 1) * P], ident[:])
                ins.then_inc(a_xnT, 1)

            def products(b, j, turn, groups):
                pe.wait_ge(ca_ld[j % 4], 16 * turn)
                pe.wait_ge(a_xt, b + 1)
                if j == 0 and groups is not None:
                    pe.wait_ge(a_grp, groups)
                w = z[:, :, P - L0_DH - L0_DH * j:2 * P - L0_DH - L0_DH * j]
                for k in range(KT):
                    first, last = j == 0 and k == 0, j == GROUP - 1 and k == KT - 1
                    pe.matmul(bank[2][:, 0:S], w[:, k], xta[:, j % 2, k],
                              start=first, stop=last)
                    ins = pe.matmul(bank[3][:, 0:S], w[:, k], ca_at(j % 4)[:, k], start=first, stop=last)
                ins.then_inc(a_mm, 1)

            transposes(0, 0, True)
            for b in range(1, GROUP):
                transposes(b, b, True)
                products(b - 1, b - 1, (b - 1) // 4 + 1, None)
            with pe.Fori(1, NG) as g:
                transposes(GROUP * g, 0, False)
                products(GROUP * g - 1, GROUP - 1, 2 * g, None)
                for j in range(1, GROUP):
                    transposes(GROUP * g + j, j, False)
                    products(GROUP * g + (j - 1), j - 1, 2 * g + ((j - 1) // 4 + 1), g)
            products(NB - 1, GROUP - 1, NB // 4, None)

            pe.wait_ge(a_grp, NG)
            for t in range(T):
                for g in range(NG):
                    ins = pe.matmul(bank[t][:, 0:S], k0t[:, g, t * P:(t + 1) * P], q0t[:, g], start=(g == 0), stop=(g == NG - 1))
            ins.then_inc(lagstep, 1)
            for t, v in enumerate((bank[4], maxb[:, 0])):
                for g in range(NG):
                    ins = pe.transpose(v[:, g * P:(g + 1) * P], k0t[:, g, t * P:(t + 1) * P], ident[:])
            ins.then_inc(v_ready, 1)
            pe.wait_ge(tern, 1)
            pe.matmul(bank[5][:, 0:3], ones[:], wabs[:], start=True, stop=True).then_inc(wsum, 1)
            pe.wait_ge(lag_dma, 16 * 3)
            for t in range(T):
                ins = pe.matmul(bank[2][0:1, 0:S], ones[:, 0:1], lagged[:, t], start=(t == 0), stop=(t == T - 1))
            ins.then_inc(lagstep, 1)
            pe.wait_ge(lag_dma, 16 * 6)
            pe.wait_ge(lagstep, L_W)
            for t in range(T):
                for k in range(T):
                    ins = pe.matmul(bank[t][:, 0:D], circ[:, k, t * P:(t + 1) * P], wout_s[:, k], start=(k == 0), stop=(k == T - 1))
            ins.then_inc(lagstep, 1)
            pe.wait_ge(lagstep, L_WMIX)
            pe.wait_ge(v_made, 1)
            for g in range(NG):
                for k in range(T):
                    ins = pe.matmul(bank[g // 2][:, (g % 2) * D:(g % 2) * D + D], v0[:, k, g * P:(g + 1) * P], wmix[:, k],
                                    start=(k == 0), stop=(k == T - 1))
            ins.then_inc(lagstep, 1)
            pipeline_may_start(pe)

            last = {}

            def use(bank_name, b, reader, k=None):
                if bank_name in last:
                    sem_, res, group, k_ = last[bank_name]
                    if b.group is None and group is not None:
                        res, group = res + NB - UNROLL, None
                    elif b.group is not None and group is None:
                        res, group = res - PEEL, b.group
                    was = batch(res, group)
                    if k_ is None:
                        after(pe, sem_, was)
                    else:
                        after4(pe, sem_, was, k_)
                last[bank_name] = (reader, b.residue, b.group, k)

            def work(o, b):
                par = b.par
                if o == 73:
                    return
                if o in (55, 56):
                    t = o - 55
                    if t == 0:
                        after4(pe, ot_made, b, 4)
                    use("d", b, on_made[t])
                    for g in range(4):
                        ins = pe.transpose(dbank[:, g * P:(g + 1) * P], ot[:, g, t * P:(t + 1) * P], ident[:])
                    ins.then_inc(otT_ready[t], 1)
                if o == 57:
                    after(pe, on_made[1], b)
                    use("d", b, otn_made)
                    for k in range(KT):
                        for t in range(T):
                            ins = pe.transpose(dbank[:, k * S + t * P:k * S + (t + 1) * P], on[:, t, k * P:(k + 1) * P], ident[:])
                    ins.then_inc(onT_ready, 1)
                if o == 58:
                    after(pe, otn_made, b)
                    use("d", b, x4_made)
                    for t in range(T):
                        for k in range(KT):
                            ins = pe.matmul(dbank[:, t * D:(t + 1) * D], otn[:, k, t * P:(t + 1) * P], wo[:, k], start=(k == 0), stop=(k == KT - 1))
                    ins.then_inc(op_ready, 1)
                if o == 60:
                    after(pe, xq_made, b)
                    use("d", b, xqt_made)
                    v = dbank[:, 0:S].bitcast(BF16)
                    for k in range(KT):
                        for t in range(T):
                            ins = pe.transpose(v[:, k * S + t * P:k * S + (t + 1) * P], xq[:, t, k * P:(k + 1) * P], identb[:])
                    ins.then_inc(xqT_ready, 1)
                if 37 <= o < 53:
                    s = o - 37
                    u, key = s // 2, (s // 2) % 2
                    if s == 0:
                        landed(pe, mx_ld, b, 32)
                        after4(pe, ex_made[3], b.ago(1), 4)
                    else:
                        after4(pe, ex_made[(s - 1) % 4], b, (s - 1) // 4 + 1)
                    for j in range(2):
                        h = 4 * (u // 2) + 2 * (s % 2) + j
                        ins = pe.matmul(cbank[:, j * S:(j + 1) * S], ks[par][0:AROWS, h, key * P:(key + 1) * P],
                                        qs[par][0:AROWS, h, :], start=True, stop=True)
                    ins.then_inc(sc_ready[s % 4], 1)
                if 39 <= o < 55 and (o - 39) % 2 == 0:
                    u = (o - 39) // 2
                    g, key = u // 2, u % 2
                    if u == 7:
                        after4(pe, ex_made[3], b, 4)
                    if u == 0:
                        after(pe, va_made, b)
                        after4(pe, ot_made, b.ago(1), 4)
                    elif key == 0:
                        after4(pe, ot_made, b, g)
                    for i in range(4):
                        ins = pe.matmul(obank[32 * i:32 * i + 32, 0:S],
                                        va[:, par, key, (4 * g + i) * 32:(4 * g + i) * 32 + 32],
                                        pt[:, (2 * u + i // 2) % 4, i % 2], start=(key == 0), stop=(key == 1))
                    ins.then_inc(pv_done[u % 2], 1)
                if 61 <= o < 69:
                    c = o - 61
                    t, n = c // 4, c % 4
                    if c == 0:
                        after(pe, xqt_made, b)
                    use("d", b, hid_made[c % 2], c // 2 + 1)
                    for i, w in enumerate((wg, wu)):
                        for k in range(KT):
                            ins = pe.matmul(dbank[:, i * 256:(i + 1) * 256], xqt[:, k, t * P:(t + 1) * P],
                                            w[:, k, n * 256:(n + 1) * 256], start=(k == 0), stop=(k == KT - 1))
                    ins.then_inc(gu_ready[c % 2], 1)
                if o in (67, 71):
                    t = (o - 67) // 4
                    after(pe, hq_made[t], b)
                    use("d", b, hqt_made[t])
                    v = dbank[:, :].bitcast(BF16)
                    for k in range(IC):
                        ins = pe.transpose(v[:, k * P:(k + 1) * P], hq[:, k * P:(k + 1) * P], identb[:])
                    ins.then_inc(hqT_ready[t], 1)
                if o in (68, 72):
                    t = (o - 68) // 4
                    after(pe, hqt_made[t], b)
                    use("d", b, out_made[t])
                    for k in range(IC):
                        ins = pe.matmul(dbank[:, 0:D], hqt[:, k], wd[:, k], start=(k == 0), stop=(k == IC - 1))
                    ins.then_inc(dn_ready[t], 1)
                if 26 <= o < 34:
                    p = o - 26
                    if p == 0:
                        landed(pe, qs_ld, b, 48)
                        landed(pe, ks_ld, b, 64)
                        after4(pe, mx_made[1], b.ago(1), 4)
                    else:
                        after4(pe, mx_made[(p - 1) % 2], b, (p - 1) // 2 + 1)
                    for t in range(T):
                        for j in range(2):
                            h = 2 * p + j
                            ins = pe.matmul(maxb[:, t, j * S:(j + 1) * S], qs[par][0:QROWS, h, t * P:(t + 1) * P],
                                            ks[par][0:QROWS, h, :], start=True, stop=True)
                    ins.then_inc(mx_ready[p % 2], 1)
                if o == 34:
                    after4(pe, mx_made[0], b, 4)
                    after4(pe, mx_made[1], b, 4)
                    use("misc", b, nml_made)
                    for t in range(T):
                        ins = pe.transpose(misc[0:H, t * P:(t + 1) * P], mx[:, t, :], ident[:])
                    ins.then_inc(mxT_ready, 1)
                if o == 20:
                    after(pe, xnb_made, b)
                    use("misc", b, xbt_made)
                    for k in range(KT):
                        for t in range(T):
                            ins = pe.transpose(misc[:, k * S + t * P:k * S + (t + 1) * P], xn[:, t, k * P:(k + 1) * P], ident[:])
                    ins.then_inc(xnb_T, 1)
                if o == 21:
                    after(pe, xbt_made, b)
                    use("misc", b, qf_made)
                    for m in range(KT):
                        for k in range(KT):
                            ins = pe.matmul(misc[:, m * S:(m + 1) * S], wq[:, k, m * P:(m + 1) * P], xbt[:, k], start=(k == 0), stop=(k == KT - 1))
                    ins.then_inc(qp_ready, 1)
                if o == 22:
                    use("misc", b, va_made)
                    for t in range(T):
                        for k in range(KT):
                            ins = pe.matmul(misc[:, t * D:(t + 1) * D], ct[:, par, k, t * P:(t + 1) * P], wv[:, k], start=(k == 0), stop=(k == KT - 1))
                    ins.then_inc(vp_ready, 1)
                if o == 5:
                    after(pe, xna_made, b)
                    use("misc", b, xal_made)
                    for k in range(KT):
                        for t in range(T):
                            ins = pe.transpose(misc[:, k * S + t * P:k * S + (t + 1) * P], xn[:, t, k * P:(k + 1) * P], ident[:])
                    ins.then_inc(xna_T, 1)
                if o == 6:
                    after(pe, xal_made, b)
                    use("misc", b, lt_made)
                    ops = [(w, v, k) for w, v in ((rwh, xah), (rwl, xah), (rwh, xal)) for k in range(KT)]
                    for i, (w, v, k) in enumerate(ops):
                        ins = pe.matmul(misc[:, 0:S], w[:, k], v[:, k], start=(i == 0), stop=(i == len(ops) - 1))
                    ins.then_inc(rt_ready, 1)
                if o == 7:
                    after(pe, lt_made, b)
                    use("misc", b, rchain, 1)
                    apart(pe, parted["pe"])
                    for t in range(T):
                        ins = pe.transpose(misc[:, t * NE:(t + 1) * NE], lt[:, t * P:(t + 1) * P], ident[0:NE, 0:NE])
                    ins.then_inc(rtt_ready, 1)
                if o == 9:
                    after4(pe, rchain2, b, 4)
                    use("misc", b, gt_made)
                    for t in range(T):
                        ins = pe.transpose(misc[0:NE, t * P:(t + 1) * P], gg[:, t], ident[:])
                    ins.then_inc(gT_ready, 1)
                if o == 10:
                    after(pe, gt_made, b)
                    use("misc", b, x3_init)
                    for t in range(T):
                        ins = pe.matmul(misc[:, t * D:(t + 1) * D], gt[:, t * P:(t + 1) * P], eb_s[:], start=True, stop=True)
                    ins.then_inc(gb_ready, 1)
                if o == 11:
                    landed(pe, c_ld, b, 16)
                    use("misc", b, kf_made)
                    for m in range(KT):
                        for k in range(KT):
                            ins = pe.matmul(misc[:, m * S:(m + 1) * S], wk[:, k, m * P:(m + 1) * P], ct[:, par, k], start=(k == 0), stop=(k == KT - 1))
                    ins.then_inc(kp_ready, 1)
                if 10 <= o < 18:
                    t, p = (o - 10) % 2, (o - 10) // 2
                    if p:
                        after4(pe, e_sum[t], b, p)
                    else:
                        after4(pe, e_sum[t], b.ago(1), 4)
                    ops = [(v, w, k) for v, w in ((xah, ewh), (xah, ewl), (xal, ewh)) for k in range(KT)]
                    for i, (v, w, k) in enumerate(ops):
                        ins = pe.matmul(ebank[t][:, :], v[:, k, t * P:(t + 1) * P], w[:, k, p * 512:(p + 1) * 512],
                                        start=(i == 0), stop=(i == len(ops) - 1))
                    ins.then_inc(e_ready[t], 1)

            pipeline(pe, work)


def kernel(x, ctx_1024, mask_Bx1xS2_ik0, L0_xattn_Wq, L0_xattn_bq, L0_xattn_Wout, L0_xattn_bout,
           L0_ffn_router_w, L0_ffn_router_b, L0_ffn_expert_w, L0_ffn_expert_b, L1_xattn_Wq, L1_xattn_bq,
           L1_xattn_Wk, L1_xattn_bk, L1_xattn_Wv, L1_xattn_bv, L1_xattn_Wo, L1_xattn_bo, L1_ffn_w_gate,
           L1_ffn_w_up, L1_ffn_w_down):
    import numpy as np
    import concourse.bacc as bacc
    from concourse.bass_utils import run_bass_kernel_spmd

    arrays = {
        "x": np.asarray(x),
        "ctxT": np.asarray(ctx_1024).transpose(0, 2, 1),
        "mask": np.asarray(mask_Bx1xS2_ik0).reshape(NB, S),
        "wq0": np.asarray(L0_xattn_Wq),
        "bq0": np.asarray(L0_xattn_bq),
        "wout_r": np.asarray(L0_xattn_Wout)[::-1],
        "bout": np.asarray(L0_xattn_bout),
        "rwT": np.asarray(L0_ffn_router_w).T,
        "rb": np.asarray(L0_ffn_router_b),
        "ewT": np.asarray(L0_ffn_expert_w).transpose(2, 0, 1).reshape(D, NE * D),
        "eb": np.asarray(L0_ffn_expert_b),
        "wqT": np.asarray(L1_xattn_Wq).T,
        "bq": np.asarray(L1_xattn_bq).reshape(KT, P).T,
        "wkT": np.asarray(L1_xattn_Wk).T,
        "bk": np.asarray(L1_xattn_bk).reshape(KT, P).T,
        "wvT": np.asarray(L1_xattn_Wv).T,
        "bv": np.asarray(L1_xattn_bv),
        "woT": np.asarray(L1_xattn_Wo).T,
        "bo": np.asarray(L1_xattn_bo),
        "wgT": np.asarray(L1_ffn_w_gate).T,
        "wuT": np.asarray(L1_ffn_w_up).T,
        "wdT": np.asarray(L1_ffn_w_down).T,
    }
    arrays = {f"in_{name}": np.ascontiguousarray(a) for name, a in arrays.items()}
    nc = bacc.Bacc("TRN2", target_bir_lowering=False, num_devices=1)
    args = [nc.dram_tensor(name, a.shape, mybir.dt.from_np(a.dtype), kind="ExternalInput").ap()
            for name, a in arrays.items()]
    args.append(nc.dram_tensor("out", (NB, S, D), F32, kind="ExternalOutput").ap())
    build(nc, *args)
    result = run_bass_kernel_spmd(nc, [arrays], core_ids=[0])
    return result.results[0]["out"]
```

```python
from contextlib import ExitStack

import concourse.bass as bass
from concourse import mybir

F32 = mybir.dt.float32
F32R = mybir.dt.float32r
BF16 = mybir.dt.bfloat16
I32 = mybir.dt.int32
U32 = mybir.dt.uint32
ALU = mybir.AluOpType
ACT = mybir.ActivationFunctionType
AX_X = mybir.AxisListType.X

P = 128
NB, S, D = 32, 256, 256
T = S // P
KT = D // P
L0_HEADS = 16
L0_DH = D // L0_HEADS
K_TOP = 12
NE = 8
H = 16
DH = D // H
INNER = 1024
IC = INNER // P
LN_EPS = 1e-5
NEG = -3.0e38
MAGIC = 12582912.0
BIG_HI, BIG_LO = 1000079360.0, -79360.0
GROUP = 8
NG = NB // GROUP
ZW = 2 * P - L0_DH
TICKS = 128
PEEL, UNROLL = 8, 4
QROWS, AROWS = 96, 98
AT = {
    "load": 0, "x2": 211, "ln_a": 190, "xn_a": 228, "xT_a": 237, "route": 232, "routeT": 226, "gate": 233,
    "gateT": 257, "gbias": 267, "expert": 266, "k": 266, "k_split": 324, "k_write": 336, "ln_b": 311,
    "xn_b": 336, "xT_b": 350, "k_read": 440, "q": 363, "q_split": 380, "v": 354, "q_write": 366,
    "q_read": 449, "max": 393, "max_T": 449, "max_row": 619, "exp": 480, "pv": 499, "out": 511, "norm": 619,
    "norm_T": 645, "o": 666, "ln_c": 650, "absmax": 649, "quant": 646, "quant_T": 658, "gate_up": 672,
    "h_max": 710, "h_quant": 703, "h_T": 711, "down": 727, "store": 675,
}
LATER = {
    "sp": {
        "k_write": -21, "store": 210, "k_read": -38, "load": 107, "q_read": -18, "q_write": 30,
        "max_row": -175,
    },
    "pool": {
        "x2": -63, "q": -5, "xn_b": -9, "xn_a": -16, "absmax": -4, "q_split": -19, "k_split": -62,
        "gate_up": -2, "o": -36, "gbias": -19,
    },
    "act": {
        "routeT": 29, "gateT": 2, "exp": 6, "k": -2, "route": 7, "xn_b": 7, "xT_b": -2, "max_T": 15,
        "gate_up": 2, "h_quant": 3, "out": 13, "quant_T": 5, "q": -3, "h_T": 9, "norm_T": -5, "xn_a": -9,
        "xT_a": -7, "quant": 15, "absmax": 11, "o": -22, "expert": 4, "gbias": -6,
    },
    "dve": {
        "routeT": 20, "k": -10, "norm": 1, "ln_a": 21, "quant": 14, "gate": 19,
        "k_split": -65, "ln_c": -6, "ln_b": 17, "max_T": 10, "v": 8, "down": 6, "h_quant": 1, "absmax": 8,
        "xT_a": -8, "expert": -3, "h_max": -12, "gate_up": -1,
    },
    "pe": {
        "xT_a": -14, "o": -31, "v": -9, "k": -18, "norm": -2, "q": -10, "norm_T": -13, "routeT": 17,
        "max": -5, "gate_up": -7, "h_T": 2, "max_T": 10, "xT_b": -6, "expert": -8, "quant_T": 3, "gateT": -8,
        "down": -2, "gbias": -16, "route": -5, "exp": -3,
    },
}
CHUNKS = {"expert": (8, 8), "max": (16, 4), "exp": (16, 8), "pv": (8, 16), "out": (4, 32), "norm": (2, 8),
          "gate_up": (8, 8), "h_max": (2, 32), "h_quant": (2, 32), "h_T": (2, 32), "down": (2, 32)}
BANKS = {
    "norm": [2, 1], "norm_T": [1], "o": [1], "quant_T": [2], "gate_up": [0, 2], "h_T": [1, 0], "down": [3, 3],
    "max_T": [3], "xT_b": [0], "q": [0], "v": [2], "xT_a": [1], "route": [3], "routeT": [0], "gateT": [2],
    "gbias": [3], "k": [0], "max": [1, 3],
}


class Batch:

    def __init__(self, n, residue, group):
        self.n, self.residue, self.group = n, residue, group
        self.par = residue % 2
        self.quad = residue % 4

    def ago(self, k):
        return batch(self.residue - k, self.group)

    @property
    def exists(self):
        return not isinstance(self.n, int) or 0 <= self.n < NB

    def turn(self):
        if self.group is None:
            return self.residue // 2 + 1
        return self.group * 2 + (self.residue // 2 + 1)

    def count(self, k, each):
        if self.group is None:
            return each * self.n + k
        return self.group * (UNROLL * each) + (each * self.residue + k)

    def fours(self, k):
        return self.count(k, 4)


def batch(residue, group):
    return Batch(residue if group is None else UNROLL * group + residue, residue, group)


def before(b, step, other):
    newer = batch(b.residue + (step - other) // TICKS, b.group)
    return batch(NB - 1, None) if b.group is None and newer.n >= NB else newer


def after(eng, sem, b):
    if b.exists:
        eng.wait_ge(sem, b.n + 1)


def after4(eng, sem, b, k):
    if b.exists:
        eng.wait_ge(sem, b.fours(k))


def after8(eng, sem, b, k):
    if b.exists:
        eng.wait_ge(sem, b.count(k, 8))


def landed(eng, sems, b, each):
    if b.exists:
        eng.wait_ge(sems[b.par], b.turn() * each)


def apart(eng, parted):
    eng.sem_inc(parted, 1)


def pipeline(eng, name, work):
    jobs = []
    for order, (job, at) in enumerate(AT.items()):
        n, apart_by = CHUNKS.get(job, (1, 0))
        for c in range(n):
            age, tick = divmod(at + LATER[name].get(job, 0) + c * apart_by, TICKS)
            jobs.append((tick, -age, order, c, job))
    jobs.sort()

    def step(residue, group):
        for _, minus_age, _, c, job in jobs:
            b = batch(residue + minus_age, group)
            if b.exists:
                work(job, c, b)

    for i in range(PEEL):
        step(i, None)
    with eng.Fori(PEEL // UNROLL, NB // UNROLL) as g:
        for j in range(UNROLL):
            step(j, g)
    for i in range(NB, NB + max(-minus_age for _, minus_age, *_ in jobs)):
        step(i, None)


def build(nc, x, ctxT, mask, wq0, bq0, wout_r, bout, rwT, rb, ewT, eb, wqT, bq, wkT, bk, wvT, bv,
          woT, bo, wgT, wuT, wdT, out):
    with ExitStack() as ctx:
        def sb(name, shape, dt=F32):
            return ctx.enter_context(nc.sbuf_tensor(name, shape, dt))

        def sem(name):
            return ctx.enter_context(nc.semaphore(name))

        def sems(name, n):
            return [sem(f"{name}{i}") for i in range(n)]

        def scratch(name, shape, dt=F32):
            return nc.dram_tensor(name, shape, dt, kind="Internal").ap()

        gram_d = scratch("gram_d", [S, 2 * S])
        lagw_d = scratch("lagw_d", [1, 2 * S])
        attn0_d = scratch("attn0_d", [NB * L0_DH, D])
        ksplit_d = scratch("ksplit_d", [2, 2, D, S])
        qsplit_d = scratch("qsplit_d", [2, 2, D, S])

        area_at = -(-nc.sbuf_base // 32) * 32
        area = sb("area", [P, 4 * H * S])
        qs = [nc.alloc_sbuf_tensor_at(f"qs{i}", [P, H, S], F32R, offset=area_at + 4 * H * S * i) for i in range(2)]
        ks = [nc.alloc_sbuf_tensor_at(f"ks{i}", [P, H, S], F32R, offset=area_at + 4 * H * S * (2 + i)) for i in range(2)]

        ident = sb("ident", [P, P])
        identb = sb("identb", [P, P], BF16)
        ones = sb("ones", [P, P])
        mhalf = sb("mhalf", [P, 2])
        magic = sb("magic", [P, 1])
        iota8 = sb("iota8", [P, NE])
        big = sb("big", [P, 1])
        wk = sb("wk", [P, KT, D])
        wq = sb("wq", [P, KT, D])
        wv = sb("wv", [P, KT, D])
        wo = sb("wo", [P, KT, D])
        bk_c = sb("bk_c", [P, KT])
        bq_c = sb("bq_c", [P, KT])
        bq4 = sb("bq4", [P, KT])
        bv_r = sb("bv_r", [P, D])
        bo_r = sb("bo_r", [P, D])
        rb_r = sb("rb_r", [P, NE])
        eb_s = sb("eb_s", [NE, D])
        rwh = sb("rwh", [P, KT, P], F32R)
        rwl = sb("rwl", [P, KT, P], F32R)
        ewh = sb("ewh", [P, KT, NE * D], F32R)
        ewl = sb("ewl", [P, KT, NE * D], F32R)
        wg = sb("wg", [P, KT, INNER], BF16)
        wu = sb("wu", [P, KT, INNER], BF16)
        wd = sb("wd", [P, IC, D], BF16)
        wabs = sb("wabs", [P, 3])
        wmean = sb("wmean", [P, 3])
        wscale = sb("wscale", [P, 3])
        hgate = sb("hgate", [P, 1])
        wup127 = sb("wup127", [P, 1])

        xl = sb("xl", [P, 2, T, D])
        a0 = sb("a0", [P, 2, D])
        ct = sb("ct", [P, 2, KT, S])
        mk = sb("mk", [P, S], I32)
        m01 = sb("m01", [P, S])
        x2 = sb("x2", [P, T, D])
        x3 = sb("x3", [P, 4, T, D])
        x4 = sb("x4", [P, 2, T, D])
        xn = sb("xn", [P, T, D])
        xah = sb("xah", [P, KT, S], F32R)
        xal = sb("xal", [P, KT, S], F32R)
        xbt = sb("xbt", [P, KT, S])
        pf = sb("pf", [P, KT, S])
        ph = sb("ph", [P, KT, S], F32R)
        pl = sb("pl", [P, KT, S], F32R)
        va = sb("va", [P, 2, T, H * 32])
        pt = sb("pt", [P, 4, 2, S])
        ot = sb("ot", [P, 4, S])
        on = sb("on", [P, T, D])
        otn = sb("otn", [P, KT, S])
        xq = sb("xq", [P, T, D], BF16)
        xqt = sb("xqt", [P, KT, S], BF16)
        th = sb("th", [P, 256])
        t1 = sb("t1", [P, 256])
        et = sb("et", [P, D])
        hid = sb("hid", [P, T, INNER])
        hq = sb("hq", [P, INNER], BF16)
        hqt = sb("hqt", [P, IC, P], BF16)
        narrow = sb("narrow", [P, S], F32R)
        nmh = narrow[0:H]
        nml = narrow[P // 2:P // 2 + H]
        mbias = narrow[3 * P // 4:3 * P // 4 + 2]
        lt = sb("lt", [NE, S])
        gt = lt
        mx = sb("mx", [P, T, H])
        bn = sb("bn", [P, 3, T, 6])
        mv = sb("mv", [P, 3, T, 2])
        ve = sb("ve", [P, 3, T])
        nm = sb("nm", [P, 3, T])
        mneg = sb("mneg", [P, 3, T])
        rs = sb("rs", [P, 3, T])
        lg = sb("lg", [P, T, NE])
        top8 = sb("top8", [P, T, 8])
        idx8 = sb("idx8", [P, T, 8], U32)
        idxf = sb("idxf", [P, T])
        ntop = sb("ntop", [P, T])
        elg = sb("elg", [P, T, NE])
        esum = sb("esum", [P, T])
        rsum = sb("rsum", [P, T])
        gg = sb("gg", [P, T, NE])
        rc = sb("rc", [P, T, H])
        am = sb("am", [P, T])
        sc = sb("sc", [P, T])
        dq = sb("dq", [P, T])
        ts_ = sb("ts_", [P, T])
        hc = sb("hc", [P, T])
        hm = sb("hm", [P, T])
        hmc = sb("hmc", [P, T])
        hmr = sb("hmr", [P, T])
        hf = sb("hf", [P, T])
        dqh = sb("dqh", [P, T])


        def part(at, *shape):
            n = 1
            for k in shape:
                n *= k
            names = "abc"[:len(shape)]
            v = area[:, at:at + n]
            if len(shape) == 1:
                return v
            return v.rearrange(f"p ({' '.join(names)}) -> p {' '.join(names)}", **dict(zip(names, shape)))

        raw_w = [part(0, 2048), part(2048, 2048), part(4096, 2048)]
        raw_e = part(6144, KT, NE * D)
        raw_r = part(10240, KT, NE)
        q0t = part(10256, NG, S)
        k0t = part(11280, NG, S)
        gram2 = part(12304, T, 2 * S)
        lagged = part(13328, T, S)
        v0 = part(13840, T, NG * P)
        circ = part(14864, T, S)
        wout_s = part(15376, T, D)
        bq0_c = part(15888, 1)
        wq_raw = part(15904, KT, L0_DH)
        xa = x3
        ca = va
        z = hid[:, 1, 0:KT * ZW].rearrange("p (k w) -> p k w", k=KT)
        xna = pt[:, 0:2]
        xta = pt[:, 2:4]
        wmix = on
        out16 = ot[:, 0:NG]
        bout_r = t1
        corr = hid[0:1, 0, 0:3 * S].rearrange("p (a s) -> p a s", a=3)
        c8 = part(15936, 4, 8)[0:1]

        def ca_at(i):
            return ca[:, i // 2, :, (i % 2) * 256:(i % 2) * 256 + 256]

        bank = [ctx.enter_context(nc.psum_tensor(f"bank{i}", [P, 512], F32)) for i in range(8)]
        ebank, cbank, obank, maxb = bank[0:2], bank[3], bank[4], bank[7]
        shared_banks = bank[2], bank[5], bank[6], bank[7]

        def shared_bank(job, c):
            return shared_banks[BANKS[job][c % len(BANKS[job])]] if job in BANKS else None

        def halves(b):
            return b[:, :].rearrange("p (a c) -> p a c", a=2)

        consts = sem("consts")
        parted = sem("parted")
        gb_out, o_out = sem("gb_out"), sem("o_out")
        e_tmp = sems("e_tmp", 2)
        early_ld, raw_ld, w_ld = sem("early_ld"), sem("raw_ld"), sem("w_ld")
        z_made = sem("z_made")
        xa_ld, ca_ld = sems("xa_ld", 4), sems("ca_ld", 4)
        a_stats, a_var, a_rstd = sem("a_stats"), sem("a_var"), sem("a_rstd")
        a_xn, a_xnT, a_xt, a_mm, a_grp = sem("a_xn"), sem("a_xnT"), sem("a_xt"), sem("a_mm"), sem("a_grp")
        lagstep = sem("lagstep")
        v_ready, v_made = sem("v_ready"), sem("v_made")
        lag_dma = sem("lag_dma")
        tern, wsum = sem("tern"), sem("wsum")
        wsplit = sem("wsplit")
        stacks_ready = sem("stacks_ready")

        x_ld, c_ld, m_ld = sems("x_ld", 2), sems("c_ld", 2), sem("m_ld")
        k_wr, q_wr, ks_ld = sems("k_wr", 2), sems("q_wr", 2), sems("ks_ld", 2)
        qs_ld, mx_ld, out_st = sems("qs_ld", 2), sems("mx_ld", 2), sems("out_st", 2)
        x2_made = sem("x2_made")
        lna_st, lna_var, lna_rstd, xna_made, xna_T = (sem("lna_st"), sem("lna_var"), sem("lna_rstd"),
                                                      sem("xna_made"), sem("xna_T"))
        lnb_st, lnb_var, lnb_rstd, xnb_made, xnb_T = (sem("lnb_st"), sem("lnb_var"), sem("lnb_rstd"),
                                                      sem("xnb_made"), sem("xnb_T"))
        xah_made, xal_made = sem("xah_made"), sem("xal_made")
        rt_ready, lt_made, rtt_ready, rchain, relg, rchain2, gT_ready, gt_made, gb_ready = (
            sem("rt_ready"), sem("lt_made"), sem("rtt_ready"), sem("rchain"), sem("relg"), sem("rchain2"),
            sem("gT_ready"), sem("gt_made"), sem("gb_ready"))
        x3_init, e_ready, e_half, e_sum = sem("x3_init"), sems("e_ready", 2), sems("e_half", 2), sems("e_sum", 2)
        m01_made, mb_made, kp_ready, kf_made, kh_made, kl_made, vp_ready, va_made = (
            sem("m01_made"), sem("mb_made"), sem("kp_ready"), sem("kf_made"), sem("kh_made"), sem("kl_made"),
            sem("vp_ready"), sem("va_made"))
        xbt_made, qp_ready, qh_made, ql_made, bo_added = (
            sem("xbt_made"), sem("qp_ready"), sem("qh_made"), sem("ql_made"), sem("bo_added"))
        mx_ready, mx_made = sems("mx_ready", 2), sems("mx_made", 2)
        mxT_ready, nmh_made, nml_made = sem("mxT_ready"), sem("nmh_made"), sem("nml_made")
        sc_ready, ex_made, pv_done, ot_made = sems("sc_ready", 4), sems("ex_made", 4), sems("pv_done", 2), sem("ot_made")
        otT_ready, rc_made, on_made = sems("otT_ready", 2), sems("rc_made", 2), sems("on_made", 2)
        onT_ready, otn_made, op_ready, x4_made = sem("onT_ready"), sem("otn_made"), sem("op_ready"), sem("x4_made")
        lnc_st, lnc_var, lnc_rstd, lnc_made = sem("lnc_st"), sem("lnc_var"), sem("lnc_rstd"), sem("lnc_made")
        rs_pow = sems("rs_pow", 3)
        qchain, qchain2, xqa_made, xq_made, xqT_ready, xqt_made = (
            sem("qchain"), sem("qchain2"), sem("xqa_made"), sem("xq_made"), sem("xqT_ready"), sem("xqt_made"))
        gu_ready, th_made, t1_made, hid_made = sems("gu_ready", 2), sems("th_made", 2), sems("t1_made", 2), sems("hid_made", 2)
        dqh_made = sem("dqh_made")
        hchain, hqa_made, hq_made, hqT_ready, hqt_made, dn_ready, out_made = (
            sems("hchain", 2), sems("hqa_made", 2), sems("hq_made", 2), sems("hqT_ready", 2),
            sems("hqt_made", 2), sems("dn_ready", 2), sems("out_made", 2))

        N_EARLY, N_RAW, N_W = 3, 5, 11
        (L_GRAM, L_GRAM2, L_CORR, L_ROW, L_TOP, L_CUT, L_NEXT, L_SENT, L_CUT2, L_SEL, L_NEGM, L_EXP,
         L_WSEL, L_SUM, L_REC, L_W, L_MIX, L_WMIX, L_OUT, L_OUT16) = range(1, 21)
        ATTN0_STORED = 16 * 7

        block = ctx.enter_context(nc.Block())

        def pipeline_may_start(eng):
            eng.wait_ge(lag_dma, ATTN0_STORED)
            eng.wait_ge(tern, 12)
            eng.wait_ge(wsplit, 5)
            eng.wait_ge(w_ld, 16 * N_W)

        @block.sync
        def _(sp):
            def early_x(b, j):
                sp.dma_start(xa[:, j], x[bass.ds(b, 1)].rearrange("o (t p) d -> (o p) t d", p=P)).then_inc(xa_ld[j], 16)

            def early_ctx(b, j):
                sp.dma_start(ca_at(j), ctxT[bass.ds(b, 1)].rearrange("o (k p) s -> (o p) k s", p=P)).then_inc(ca_ld[j], 16)

            def early_turn(g, j):
                sp.wait_ge(a_xn, 4 * g + (j - 3))
                early_x(4 * g + j, j)
                if isinstance(g, int) and g == 1 and j == 0:
                    return
                sp.wait_ge(a_mm, 4 * g + (j - 4))
                early_ctx(4 * g + (j - 1), (j - 1) % 4)

            for b in range(2):
                early_x(b, b)
            sp.dma_start(bq0_c, bass.AP(bq0.tensor, 0, [[0, GROUP], [1, L0_DH], [1, 1]])).then_inc(early_ld, 16)
            sp.dma_start(wq_raw, wq0.rearrange("(k p) n -> p k n", p=P)).then_inc(early_ld, 16)
            sp.dma_start(wout_s, wout_r.rearrange("(k p) n -> p k n", p=P)).then_inc(early_ld, 16)
            for b in range(4):
                if b >= 2:
                    early_x(b, b)
                early_ctx(b, b)
            for src, dst in ((wgT, raw_w[0]), (wuT, raw_w[1])):
                sp.dma_start(dst.rearrange("p (k n) -> p k n", k=KT), src.rearrange("(k p) n -> p k n", p=P)).then_inc(raw_ld, 16)
            sp.dma_start(raw_w[2].rearrange("p (k n) -> p k n", k=IC), wdT.rearrange("(k p) n -> p k n", p=P)).then_inc(raw_ld, 16)
            sp.dma_start(raw_e, ewT.rearrange("(k p) n -> p k n", p=P)).then_inc(raw_ld, 16)
            sp.dma_start(raw_r, rwT.rearrange("(k p) n -> p k n", p=P)).then_inc(raw_ld, 16)
            for j in range(4):
                early_turn(1, j)
            with sp.Fori(2, NB // 4) as g:
                for j in range(4):
                    early_turn(g, j)
            sp.wait_ge(a_mm, NB - 4)
            early_ctx(NB - 1, 3)
            for dst, src in ((wq, wqT), (wk, wkT), (wv, wvT), (wo, woT)):
                sp.dma_start(dst[:], src.rearrange("(k p) n -> p k n", p=P)).then_inc(w_ld, 16)
            for dst, src in ((bq_c, bq), (bk_c, bk)):
                sp.dma_start(dst[:], src).then_inc(w_ld, 16)
            for dst, src, n in ((bv_r, bv, D), (bo_r, bo, D), (rb_r, rb, NE)):
                sp.dma_start(dst[:], bass.AP(src.tensor, 0, [[0, P], [1, n]])).then_inc(w_ld, 16)
            sp.dma_start(eb_s[:], eb).then_inc(w_ld, 16)
            sp.dma_start(bout_r[:], bass.AP(bout.tensor, 0, [[0, P], [1, D]])).then_inc(w_ld, 16)

            sp.wait_ge(lagstep, L_GRAM2)
            sp.dma_start(gram_d.rearrange("(t p) m -> p t m", p=P), gram2).then_inc(lag_dma, 16)
            sp.wait_ge(lag_dma, 16)
            for t in range(T):
                sp.dma_start(lagged[:, t], bass.AP(gram_d.tensor, t * P * (2 * S + 1), [[2 * S + 1, P], [1, S]]))\
                    .then_inc(lag_dma, 16)
            sp.wait_ge(lagstep, L_W)
            for i in range(2):
                sp.dma_start(lagw_d[:, i * S:(i + 1) * S], corr[:, 2, :]).then_inc(lag_dma, 16)
            sp.wait_ge(lag_dma, 16 * 5)
            sp.dma_start(circ, bass.AP(lagw_d.tensor, 1, [[1, P], [P, T], [1, S]])).then_inc(lag_dma, 16)
            sp.wait_ge(lagstep, L_OUT16)
            sp.dma_start(attn0_d.rearrange("(g p) d -> p g d", p=P), out16[:]).then_inc(lag_dma, 16)
            pipeline_may_start(sp)

            def work(job, c, b):
                if job == "load":
                    after(sp, x2_made, b.ago(2))
                    sp.dma_start(xl[:, b.par], x[bass.ds(b.n, 1)].rearrange("o (t p) d -> (o p) t d", p=P))\
                        .then_inc(x_ld[b.par], 16)
                    rows = attn0_d.rearrange("(b r) d -> b r d", r=L0_DH)[bass.ds(b.n, 1)]
                    sp.dma_start(a0[:, b.par], bass.AP(rows.tensor, rows.offset, [[0, P // L0_DH], [D, L0_DH], [1, D]],
                                                       runtime_checks=rows.runtime_checks)).then_inc(x_ld[b.par], 16)
                    after(sp, vp_ready, b.ago(2))
                    sp.dma_start(ct[:, b.par], ctxT[bass.ds(b.n, 1)].rearrange("o (k p) s -> (o p) k s", p=P))\
                        .then_inc(c_ld[b.par], 16)
                    after(sp, m01_made, b.ago(1))
                    row = mask[bass.ds(b.n, 1)]
                    sp.dma_start(mk[:], bass.AP(row.tensor, row.offset, [[0, P], [1, S]],
                                                runtime_checks=row.runtime_checks)).then_inc(m_ld, 16)
                if job == "k_write":
                    after(sp, kl_made, b)
                    apart(sp, parted)
                    landed(sp, ks_ld, b.ago(2), 64)
                    for i, src in enumerate((ph, pl)):
                        sp.dma_start(ksplit_d[b.par, i].rearrange("(k p) s -> p k s", p=P), src[:].bitcast(F32)).then_inc(k_wr[b.par], 16)
                if job == "k_read":
                    landed(sp, k_wr, b, 32)
                    apart(sp, parted)
                    after4(sp, sc_ready[3], b.ago(2), 4)
                    if b.residue < 2 and b.group is None:
                        sp.wait_ge(stacks_ready, 7)
                    for row, i in ((0, 0), (DH, 0), (2 * DH, 1)):
                        sp.dma_start(ks[b.par][row:row + DH].bitcast(F32), ksplit_d[b.par, i].rearrange("(h d) s -> d h s", d=DH))\
                            .then_inc(ks_ld[b.par], 16)
                    after(sp, mb_made, b)
                    sp.dma_start(ks[b.par][3 * DH:3 * DH + 2].bitcast(F32), mbias.bitcast(F32).unsqueeze(1).to_broadcast([2, H, S]))\
                        .then_inc(ks_ld[b.par], 16)
                if job == "q_write":
                    after(sp, ql_made, b)
                    apart(sp, parted)
                    landed(sp, qs_ld, b.ago(2), 48)
                    for i, src in enumerate((ph, pl)):
                        sp.dma_start(qsplit_d[b.par, i].rearrange("(k p) s -> p k s", p=P), src[:].bitcast(F32)).then_inc(q_wr[b.par], 16)
                if job == "q_read":
                    landed(sp, q_wr, b, 32)
                    apart(sp, parted)
                    after4(sp, sc_ready[3], b.ago(2), 4)
                    for row, i in ((0, 0), (DH, 1), (2 * DH, 0)):
                        sp.dma_start(qs[b.par][row:row + DH].bitcast(F32), qsplit_d[b.par, i].rearrange("(h d) s -> d h s", d=DH))\
                            .then_inc(qs_ld[b.par], 16)
                if job == "max_row":
                    after(sp, nml_made, b)
                    for i, src in enumerate((nmh, nml)):
                        sp.dma_start(qs[b.par][QROWS + i:QROWS + i + 1].bitcast(F32), src.bitcast(F32)).then_inc(mx_ld[b.par], 16)
                if job == "store":
                    after(sp, out_made[1], b)
                    sp.dma_start(out[bass.ds(b.n, 1)].rearrange("o (t p) d -> (o p) t d", p=P), x4[:, b.par]).then_inc(out_st[b.par], 16)

            pipeline(sp, "sp", work)
            for i in range(2):
                sp.wait_ge(out_st[i], 16 * (NB // 2))

        @block.gpsimd
        def _(pool):
            pool.memset(ident[:], 0.0)
            pool.memset(ones[:], 1.0)
            pool.memset(mhalf[:], -0.5)
            pool.memset(magic[:], MAGIC)
            pool.memset(z, 0.0)
            for e in range(NE - 1):
                pool.memset(iota8[:, e:e + 1], float(e))
            pool.memset(iota8[:, NE - 1:NE], float(NE - 1)).then_inc(consts, 1)
            pool.wait_ge(consts, 1)
            pool.memset(big[96:98, :], BIG_LO).then_inc(consts, 1)
            pool.wait_ge(consts, 2)
            pool.memset(big[96:97, :], BIG_HI).then_inc(consts, 1)
            pool.wait_ge(consts, 3)
            pool.affine_select(out=ident[:], in_=ident[:], compare_op=ALU.not_equal, fill=1.0, base=0,
                               pattern=[[-1, P]], channel_multiplier=1).then_inc(consts, 1)
            pool.wait_ge(consts, 4)
            pool.tensor_copy(identb[:], ident[:]).then_inc(consts, 1)

            def rstd(b, j):
                pool.wait_ge(a_var, b + 1)
                pool.tensor_tensor(rs[:, j], ve[:, j], mhalf[:], ALU.pow).then_inc(a_rstd, 1)

            for b in range(2):
                rstd(b, b % 2)
            with pool.Fori(1, NB // 2) as g:
                for j in range(2):
                    rstd(2 * g + j, j)

            pool.wait_ge(raw_ld, 16 * N_RAW)
            pool.tensor_scalar(ewh[:], raw_e, 1.0, None, ALU.mult).then_inc(wsplit, 1)
            pool.memset(rwh[:].bitcast(F32), 0.0)
            pool.memset(rwl[:].bitcast(F32), 0.0).then_inc(wsplit, 1)
            pool.wait_ge(wsplit, 2)
            pool.tensor_scalar(rwh[:, :, 0:NE], raw_r, 1.0, None, ALU.mult).then_inc(wsplit, 1)
            pool.tensor_tensor(ewl[:], raw_e, ewh[:].bitcast(F32), ALU.subtract).then_inc(wsplit, 1)
            pool.wait_ge(wsplit, 4)
            pool.tensor_tensor(rwl[:, :, 0:NE], raw_r, rwh[:, :, 0:NE].bitcast(F32), ALU.subtract).then_inc(wsplit, 1)
            pipeline_may_start(pool)

            def stacks():
                pool.memset(va[:], 1.0).then_inc(stacks_ready, 1)
                for i in range(2):
                    pool.memset(qs[i][:].bitcast(F32), 0.0).then_inc(stacks_ready, 1)
                    pool.memset(ks[i][:].bitcast(F32), 0.0).then_inc(stacks_ready, 1)
                pool.wait_ge(stacks_ready, 5)
                for i in range(2):
                    pool.memset(ks[i][QROWS:P].bitcast(F32), 1.0)
                    pool.memset(qs[i][32:64].bitcast(F32), 1.0).then_inc(stacks_ready, 1)
                pool.wait_ge(stacks_ready, 7)

            def rstd_of(i, b, made):
                pool.tensor_tensor(rs[:, i], ve[:, i], mhalf[:], ALU.pow).then_inc(rs_pow[i], 1)
                after(pool, rs_pow[i], b)
                pool.tensor_tensor(nm[:, i], mneg[:, i], rs[:, i], ALU.mult).then_inc(made, 1)

            def work(job, c, b):
                if job == "x2":
                    landed(pool, x_ld, b, 32)
                    after(pool, x3_init, before(b, AT["x2"], AT["gbias"]))
                    pool.tensor_tensor(x2[:], xl[:, b.par], a0[:, b.par].unsqueeze(1).to_broadcast([P, T, D]),
                                       ALU.add).then_inc(x2_made, 1)
                    if b.group is None and b.residue == 0:
                        stacks()
                if job == "xn_a":
                    after(pool, lna_var, b)
                    after(pool, xna_made, b.ago(1))
                    rstd_of(0, b, lna_rstd)
                if job == "gbias":
                    after(pool, gb_out, b)
                    pool.tensor_tensor(x3[:, b.quad], x3[:, b.quad], x2[:], ALU.add).then_inc(x3_init, 1)
                if job == "expert":
                    t, p = c % 2, c // 2
                    after4(pool, e_tmp[t], b, p + 1)
                    pool.tensor_tensor(x3[:, b.quad, t], x3[:, b.quad, t], et[:], ALU.add).then_inc(e_sum[t], 1)
                if job == "gate_up":
                    part_ = hid[:, c // 4, (c % 4) * 256:(c % 4) * 256 + 256]
                    after4(pool, t1_made[c % 2], b, c // 2 + 1)
                    pool.tensor_tensor(part_, part_, t1[:], ALU.mult).then_inc(hid_made[c % 2], 1)
                if job == "o":
                    after(pool, o_out, b)
                    after(pool, bo_added, b)
                    pool.tensor_tensor(x4[:, b.par], x4[:, b.par], x3[:, b.quad], ALU.add).then_inc(x4_made, 1)
                if job == "k_split":
                    after(pool, kh_made, b)
                    after(pool, kf_made, b)
                    landed(pool, q_wr, before(b, AT["k_split"], AT["q_write"]), 32)
                    pool.tensor_tensor(pl[:], pf[:], ph[:].bitcast(F32), ALU.subtract).then_inc(kl_made, 1)
                if job == "xn_b":
                    after(pool, lnb_var, b)
                    after(pool, xnb_made, b.ago(1))
                    rstd_of(1, b, lnb_rstd)
                if job == "q":
                    after(pool, xnb_made, b)
                    pool.tensor_tensor(x3[:, b.quad], x3[:, b.quad], bo_r[:].unsqueeze(1).to_broadcast([P, T, D]),
                                       ALU.add).then_inc(bo_added, 1)
                if job == "q_split":
                    after(pool, qh_made, b)
                    landed(pool, k_wr, before(b, AT["q_split"], AT["k_write"]), 32)
                    pool.tensor_tensor(pl[:], pf[:], ph[:].bitcast(F32), ALU.subtract).then_inc(ql_made, 1)
                if job == "absmax":
                    after(pool, lnc_var, b)
                    after(pool, lnc_made, b.ago(1))
                    rstd_of(2, b, lnc_rstd)

            pipeline(pool, "pool", work)

        @block.scalar
        def _(act):
            act.wait_ge(early_ld, 16 * N_EARLY)

            def evacuate(b, j):
                act.wait_ge(a_xnT, b + 1)
                if not (isinstance(b, int) and b < 2):
                    act.wait_ge(a_mm, b - 1)
                act.activation(xta[:, j % 2], halves(bank[j % 2]), ACT.Copy).then_inc(a_xt, 1)

            def group_out(g, n):
                act.wait_ge(a_mm, n)
                act.activation(q0t[:, g], bank[2][:, 0:S], ACT.Identity, bias=bq0_c)
                act.activation(k0t[:, g], bank[3][:, 0:S], ACT.Identity, bias=bq0_c).then_inc(a_grp, 1)

            for b in range(GROUP):
                evacuate(b, b)
            with act.Fori(1, NG) as g:
                evacuate(GROUP * g, 0)
                act.wait_ge(a_mm, GROUP * g)
                act.activation(q0t.rearrange("p g s -> p (g s)")[:, bass.ds(g * S - S, S)], bank[2][:, 0:S],
                               ACT.Identity, bias=bq0_c)
                act.activation(k0t.rearrange("p g s -> p (g s)")[:, bass.ds(g * S - S, S)], bank[3][:, 0:S],
                               ACT.Identity, bias=bq0_c).then_inc(a_grp, 1)
                for j in range(1, GROUP):
                    evacuate(GROUP * g + j, j)
            group_out(NG - 1, NB)

            act.wait_ge(lagstep, L_GRAM)
            for t in range(T):
                act.activation(gram2[:, t, 0:S], bank[t][:, 0:S], ACT.Copy)
                ins = act.activation(gram2[:, t, S:2 * S], bank[t][:, 0:S], ACT.Copy)
            ins.then_inc(lagstep, 1)
            act.wait_ge(v_ready, 1)
            act.activation(v0[:, 0], bank[4][:, 0:NG * P], ACT.Copy)
            act.activation(v0[:, 1], maxb[:, 0:NG * P], ACT.Copy).then_inc(v_made, 1)
            act.wait_ge(lagstep, L_NEGM)
            act.activation(corr[:, 2, :], corr[:, 0, :], ACT.Exp, bias=c8[:, 3, 0:1]).then_inc(lagstep, 1)
            act.wait_ge(lagstep, L_MIX)
            for t in range(T):
                ins = act.activation(wmix[:, t], bank[t][:, 0:D], ACT.Copy)
            ins.then_inc(lagstep, 1)
            pipeline_may_start(act)

            def work(job, c, b):
                shared = shared_bank(job, c)
                if job in ("xn_a", "xn_b", "absmax"):
                    if job == "xn_a":
                        i, src, dst, made = 0, x2, xn, xna_made
                        after(act, lna_rstd, b)
                        after(act, xnb_T, before(b, AT["xn_a"], AT["xT_b"]))
                    elif job == "xn_b":
                        i, src, dst, made = 1, x3[:, b.quad], xn, xnb_made
                        after(act, lnb_rstd, b)
                        after(act, xna_T, before(b, AT["xn_b"], AT["xT_a"]))
                    else:
                        i, src, dst, made = 2, x4[:, b.par], on, lnc_made
                        after(act, lnc_rstd, b)
                    for t in range(T):
                        ins = act.activation(dst[:, t], src[:, t], ACT.Identity, bias=nm[:, i, t:t + 1],
                                             scale=rs[:, i, t:t + 1])
                    ins.then_inc(made, 1)
                if job == "xT_a":
                    after(act, xna_T, b)
                    after4(act, e_ready[1], before(b, AT["xT_a"], AT["expert"] + 56), 4)
                    act.activation(xah[:], halves(shared), ACT.Copy).then_inc(xah_made, 1)
                if job == "route":
                    after(act, rt_ready, b)
                    after(act, gb_ready, b.ago(1))
                    act.activation(lt[:], shared[0:NE, 0:S], ACT.Copy).then_inc(lt_made, 1)
                if job == "routeT":
                    after4(act, rchain, b, 3)
                    after4(act, rchain2, b.ago(1), 4)
                    for t in range(T):
                        ins = act.activation(elg[:, t], lg[:, t], ACT.Exp, bias=ntop[:, t:t + 1],
                                             accum_out=esum[:, t:t + 1])
                    ins.then_inc(relg, 1)
                if job == "gateT":
                    after(act, gT_ready, b)
                    act.activation(gt[:], shared[0:NE, 0:S], ACT.Copy).then_inc(gt_made, 1)
                if job == "gbias":
                    after(act, gb_ready, b)
                    after(act, x4_made, b.ago(4))
                    act.activation(x3[:, b.quad], halves(shared), ACT.Copy).then_inc(gb_out, 1)
                if job == "k":
                    after(act, kf_made, b)
                    landed(act, q_wr, before(b, AT["k"], AT["q_write"]), 32)
                    act.activation(ph[:], pf[:], ACT.Copy).then_inc(kh_made, 1)
                if job == "xT_b":
                    after(act, xnb_T, b)
                    after(act, qp_ready, b.ago(1))
                    act.activation(xbt[:], halves(shared), ACT.Copy).then_inc(xbt_made, 1)
                if job == "q":
                    after(act, qp_ready, b)
                    after(act, kl_made, before(b, AT["q"], AT["k_split"]))
                    landed(act, k_wr, before(b, AT["q"], AT["k_write"]), 32)
                    for dst in (pf, ph):
                        for m in range(KT):
                            ins = act.activation(dst[:, m], shared[:, m * S:(m + 1) * S], ACT.Identity,
                                                 bias=bq4[:, m:m + 1], scale=0.25)
                    ins.then_inc(qh_made, 1)
                if job == "max_T":
                    after(act, mxT_ready, b)
                    landed(act, mx_ld, b.ago(1), 32)
                    act.activation(nmh, shared[0:H, 0:S], ACT.Copy, scale=-1.0).then_inc(nmh_made, 1)
                if job == "exp":
                    s = c
                    after4(act, sc_ready[s % 4], b, s // 4 + 1)
                    u = s // 2 - 2
                    if u >= 0:
                        after4(act, pv_done[u % 2], b, u // 2 + 1)
                    else:
                        after4(act, pv_done[u % 2], b.ago(1), (u + 8) // 2 + 1)
                    act.activation(pt[:, s % 4].rearrange("p a c -> p (a c)"), cbank[:, :], ACT.Exp).then_inc(ex_made[s % 4], 1)
                if job == "out":
                    g = c
                    after4(act, pv_done[1], b, g + 1)
                    if g == 0:
                        after(act, otT_ready[1], b.ago(1))
                    act.activation(ot[:, g], obank[:, 0:S], ACT.Copy).then_inc(ot_made, 1)
                if job == "norm_T":
                    after(act, onT_ready, b)
                    after(act, op_ready, b.ago(1))
                    act.activation(otn[:], halves(shared), ACT.Copy).then_inc(otn_made, 1)
                if job == "o":
                    after(act, op_ready, b)
                    if b.ago(2).exists:
                        act.wait_ge(out_st[b.par], b.turn() * 16 - 16)
                    act.activation(x4[:, b.par], halves(shared), ACT.Copy).then_inc(o_out, 1)
                if job == "quant":
                    after4(act, qchain, b, 3)
                    for t in range(T):
                        ins = act.activation(on[:, t], on[:, t], ACT.Identity, bias=magic[:], scale=sc[:, t:t + 1])
                    ins.then_inc(xqa_made, 1)
                if job == "quant_T":
                    after(act, xqT_ready, b)
                    after4(act, gu_ready[1], b.ago(1), 4)
                    act.activation(xqt[:].rearrange("p k s -> p (k s)"), shared[:, 0:S].bitcast(BF16), ACT.Copy)\
                        .then_inc(xqt_made, 1)
                if job == "expert":
                    t, p = c % 2, c // 2
                    after4(act, e_half[t], b, p + 1)
                    if c:
                        after4(act, e_sum[1 - t], b, (c - 1) // 2 + 1)
                    else:
                        after4(act, e_sum[1], b.ago(1), 4)
                    act.activation(et[:], ebank[t][:, D:2 * D], ACT.Copy, scale=gg[:, t, 2 * p + 1:2 * p + 2])\
                        .then_inc(e_tmp[t], 1)
                if job == "gate_up":
                    after4(act, gu_ready[c % 2], b, c // 2 + 1)
                    if c % 4 == 0:
                        after(act, hq_made[c // 4], b.ago(1))
                    act.activation(hid[:, c // 4, (c % 4) * 256:(c % 4) * 256 + 256], shared[:, 256:512], ACT.Copy)
                    if c:
                        after4(act, t1_made[(c - 1) % 2], b, (c - 1) // 2 + 1)
                    else:
                        after4(act, t1_made[1], b.ago(1), 4)
                    after4(act, qchain, b, 4)
                    act.activation(th[:], shared[:, 0:256], ACT.Tanh, scale=ts_[:, c // 4:c // 4 + 1])\
                        .then_inc(th_made[c % 2], 1)
                if job == "h_quant":
                    t = c
                    after4(act, hchain[t], b, 4)
                    act.activation(hid[:, t], hid[:, t], ACT.Identity, bias=magic[:], scale=hf[:, t:t + 1])\
                        .then_inc(hqa_made[t], 1)
                if job == "h_T":
                    t = c
                    after(act, hqT_ready[t], b)
                    after(act, dn_ready[1 - t], b if t else b.ago(1))
                    act.activation(hqt[:].rearrange("p k s -> p (k s)"), shared[:, :].bitcast(BF16), ACT.Copy)\
                        .then_inc(hqt_made[t], 1)

            pipeline(act, "act", work)

        @block.vector
        def _(dve):
            def stats(src, i, st, var, b, n):
                for t in range(T):
                    dve.bn_stats(bn[:, i, t], src[:, t]).then_inc(st, 1)
                for t in range(T):
                    dve.wait_ge(st, n(t + 1))
                    apart(dve, parted)
                    dve.bn_aggr(mv[:, i, t], bn[:, i, t]).then_inc(st, 1)
                dve.wait_ge(st, n(4))
                dve.tensor_scalar(mneg[:, i], mv[:, i, :, 0], -1.0, None, ALU.mult)
                dve.tensor_scalar(ve[:, i], mv[:, i, :, 1], LN_EPS, None, ALU.add).then_inc(var, 1)

            dve.wait_ge(consts, 5)
            dve.wait_ge(early_ld, 16 * N_EARLY)
            dve.tensor_copy(z[:, :, P - L0_DH:P], wq_raw).then_inc(z_made, 1)

            def early(b, j, turn, first):
                if first and j < 2:
                    pass
                else:
                    dve.wait_ge(a_xn, b - 1)
                    dve.wait_ge(a_rstd, b - 1)
                dve.wait_ge(xa_ld[j % 4], 16 * turn)
                stats(xa[:, j % 4], j % 2, a_stats, a_var, b, lambda k: 4 * b + k)

            def apply(b, j, first):
                dve.wait_ge(a_rstd, b + 1)
                if not (first and j < 2):
                    dve.wait_ge(a_xnT, b - 1)
                for t in range(T):
                    ins = dve.tensor_scalar(xna[:, j % 2, t], xa[:, j % 4, t], mv[:, j % 2, t, 0:1],
                                            rs[:, j % 2, t:t + 1], ALU.subtract, ALU.mult)
                ins.then_inc(a_xn, 1)

            for b in range(4):
                early(b, b, 1, True)
                if b:
                    apply(b - 1, b - 1, True)
            with dve.Fori(1, NB // 4) as g:
                for j in range(4):
                    early(4 * g + j, j, g + 1, False)
                    apply(4 * g + (j - 1), (j - 1) % 4, False)
            apply(NB - 1, 3, False)

            dve.wait_ge(raw_ld, 16 * N_RAW)
            for i in range(3):
                ins = dve.tensor_reduce(wabs[:, i:i + 1], raw_w[i], AX_X, ALU.add, apply_absolute_value=True)
            ins.then_inc(tern, 1)
            dve.wait_ge(wsum, 1)
            dve.tensor_scalar(wmean[:], bank[5][:, 0:3], 1.0 / (D * INNER), 1e-5, ALU.mult, ALU.max).then_inc(tern, 1)
            dve.wait_ge(tern, 2)
            dve.tensor_scalar(hgate[:], wmean[:, 0:1], 0.5, None, ALU.mult)
            dve.tensor_scalar(wup127[:], wmean[:, 1:2], 1.0 / 127.0, None, ALU.mult)
            dve.reciprocal(wscale[:], wmean[:]).then_inc(tern, 1)
            dve.wait_ge(tern, 3)
            for i in range(3):
                dve.tensor_scalar(raw_w[i], raw_w[i], wscale[:, i:i + 1], -1.0, ALU.mult, ALU.max).then_inc(tern, 1)

            dve.wait_ge(lagstep, L_CORR)
            dve.tensor_scalar(corr[:, 0, :], bank[2][0:1, 0:S], 1.0 / (NB * L0_DH), None, ALU.mult).then_inc(lagstep, 1)
            dve.wait_ge(lagstep, L_ROW)
            dve.max(c8[:, 0, :], corr[:, 0, :]).then_inc(lagstep, 1)
            dve.wait_ge(lagstep, L_TOP)
            dve.match_replace(corr[:, 1, :], c8[:, 0, :], corr[:, 0, :], NEG).then_inc(lagstep, 1)
            dve.wait_ge(lagstep, L_CUT)
            dve.max(c8[:, 1, :], corr[:, 1, :]).then_inc(lagstep, 1)
            dve.wait_ge(lagstep, L_NEXT)
            dve.memset(c8[:, 1, K_TOP - 8:8], NEG).then_inc(lagstep, 1)
            dve.wait_ge(lagstep, L_SENT)
            dve.match_replace(corr[:, 1, :], c8[:, 1, :], corr[:, 1, :], NEG).then_inc(lagstep, 1)
            dve.wait_ge(lagstep, L_CUT2)
            dve.tensor_scalar(corr[:, 1, :], corr[:, 1, :], NEG, None, ALU.is_equal).then_inc(lagstep, 1)
            dve.wait_ge(lagstep, L_SEL)
            dve.tensor_scalar(c8[:, 3, 0:1], c8[:, 0, 0:1], -1.0, None, ALU.mult).then_inc(lagstep, 1)
            dve.wait_ge(lagstep, L_EXP)
            dve.tensor_tensor(corr[:, 2, :], corr[:, 2, :], corr[:, 1, :], ALU.mult).then_inc(lagstep, 1)
            dve.wait_ge(lagstep, L_WSEL)
            dve.tensor_reduce(c8[:, 2, 0:1], corr[:, 2, :], AX_X, ALU.add).then_inc(lagstep, 1)
            dve.wait_ge(lagstep, L_SUM)
            dve.reciprocal(c8[:, 2, 1:2], c8[:, 2, 0:1]).then_inc(lagstep, 1)
            dve.wait_ge(lagstep, L_REC)
            dve.tensor_scalar(corr[:, 2, :], corr[:, 2, :], c8[:, 2, 1:2], None, ALU.mult).then_inc(lagstep, 1)

            for i in range(3):
                dve.wait_ge(tern, 4 + i)
                dve.tensor_scalar(raw_w[i], raw_w[i], 1.0, MAGIC, ALU.min, ALU.add).then_inc(tern, 1)
            dve.wait_ge(w_ld, 16 * N_W)
            dve.tensor_scalar(bq4[:], bq_c[:], 0.25, None, ALU.mult)
            for i, w in enumerate((wg, wu, wd)):
                dve.wait_ge(tern, 7 + i)
                dve.tensor_scalar(w[:].rearrange("p k n -> p (k n)"), raw_w[i], MAGIC, None, ALU.subtract).then_inc(tern, 1)
            dve.wait_ge(lagstep, L_OUT)
            for g in range(NG):
                b_ = bank[g // 2][:, (g % 2) * D:(g % 2) * D + D]
                ins = dve.tensor_tensor(out16[:, g], b_, bout_r[:], ALU.add)
            ins.then_inc(lagstep, 1)
            pipeline_may_start(dve)

            def work(job, c, b):
                shared = shared_bank(job, c)
                if job == "ln_a":
                    after(dve, x2_made, b)
                    after(dve, xna_made, b.ago(1))
                    stats(x2, 0, lna_st, lna_var, b, b.fours)
                if job == "xT_a":
                    after(dve, xah_made, b)
                    dve.tensor_tensor(xal[:], halves(shared), xah[:].bitcast(F32), ALU.subtract).then_inc(xal_made, 1)
                    dve.wait_ge(m_ld, b.n * 16 + 16)
                    after(dve, kf_made, b.ago(1))
                    dve.tensor_scalar(m01[:], mk[:], 0, None, ALU.not_equal).then_inc(m01_made, 1)
                if job == "k_split":
                    after(dve, m01_made, b)
                    landed(dve, ks_ld, before(b, AT["k_split"], AT["k_read"]), 64)
                    dve.tensor_scalar(mbias, m01[96:98], 1.0, big[96:98, 0:1], ALU.subtract, ALU.mult).then_inc(mb_made, 1)
                if job == "routeT":
                    after(dve, rtt_ready, b)
                    after(dve, relg, b.ago(1))
                    dve.tensor_tensor(lg[:], shared[:, 0:T * NE].rearrange("p (t e) -> p t e", e=NE),
                                      rb_r[:].unsqueeze(1).to_broadcast([P, T, NE]), ALU.add).then_inc(rchain, 1)
                    after4(dve, rchain, b, 1)
                    apart(dve, parted)
                    for t in range(T):
                        ins = dve.max(top8[:, t], lg[:, t])
                    ins.then_inc(rchain, 1)
                    after4(dve, rchain, b, 2)
                    dve.tensor_scalar(ntop[:], top8[:, :, 0], -1.0, None, ALU.mult).then_inc(rchain, 1)
                    apart(dve, parted)
                    for t in range(T):
                        ins = dve.max_index(idx8[:, t], top8[:, t], lg[:, t])
                    ins.then_inc(rchain, 1)
                    after4(dve, rchain, b, 4)
                    dve.tensor_copy(idxf[:], idx8[:, :, 0]).then_inc(rchain2, 1)
                if job == "gate":
                    after(dve, relg, b)
                    dve.reciprocal(rsum[:], esum[:]).then_inc(rchain2, 1)
                    after4(dve, rchain2, b, 2)
                    after(dve, gT_ready, b.ago(1))
                    after4(dve, e_sum[1], b.ago(1), 4)
                    for t in range(T):
                        dve.tensor_scalar(gg[:, t], iota8[:], idxf[:, t:t + 1], rsum[:, t:t + 1],
                                          ALU.is_equal, ALU.mult).then_inc(rchain2, 1)
                if job == "expert":
                    t, p = c % 2, c // 2
                    after4(dve, e_ready[t], b, p + 1)
                    if p == 0:
                        after(dve, x3_init, b)
                    else:
                        after4(dve, e_sum[t], b, p)
                    dve.scalar_tensor_tensor(out=x3[:, b.quad, t], in0=ebank[t][:, 0:D],
                                             scalar=gg[:, t, 2 * p:2 * p + 1], in1=x3[:, b.quad, t],
                                             op0=ALU.mult, op1=ALU.add).then_inc(e_half[t], 1)
                if job == "k":
                    after(dve, kp_ready, b)
                    after(dve, ql_made, before(b, AT["k"], AT["q_split"]))
                    for m in range(KT):
                        ins = dve.scalar_tensor_tensor(out=pf[:, m], in0=shared[:, m * S:(m + 1) * S],
                                                       scalar=bk_c[:, m:m + 1], in1=m01[:], op0=ALU.add, op1=ALU.mult)
                    ins.then_inc(kf_made, 1)
                if job == "ln_b":
                    for t in range(T):
                        after4(dve, e_sum[t], b, 4)
                    after(dve, xnb_made, b.ago(1))
                    stats(x3[:, b.quad], 1, lnb_st, lnb_var, b, b.fours)
                if job == "v":
                    after(dve, vp_ready, b)
                    after4(dve, pv_done[1], b.ago(2), 4)
                    if b.group is None and b.residue < 2:
                        dve.wait_ge(stacks_ready, 7)
                    v = va[:, b.par].rearrange("p t (h c) -> p t h c", c=32)
                    for t in range(T):
                        ins = dve.tensor_tensor(v[:, t, :, 0:DH], shared[:, t * D:(t + 1) * D].rearrange("p (h c) -> p h c", c=DH),
                                                bv_r[:].rearrange("p (h c) -> p h c", c=DH), ALU.add)
                    ins.then_inc(va_made, 1)
                if job == "max":
                    p, t = c // 2, c % 2
                    after8(dve, mx_ready[t], b, p + 1)
                    if c == 0:
                        after(dve, mxT_ready, b.ago(1))
                    dve.tensor_reduce(mx[:, t, 2 * p:2 * p + 2], shared[:].rearrange("p (h s) -> p h s", h=2),
                                      AX_X, ALU.max).then_inc(mx_made[t], 1)
                if job == "max_T":
                    after(dve, nmh_made, b)
                    dve.scalar_tensor_tensor(out=nml, in0=shared[0:H, 0:S], scalar=-1.0, in1=nmh.bitcast(F32),
                                             op0=ALU.mult, op1=ALU.subtract).then_inc(nml_made, 1)
                if job == "norm":
                    t = c
                    after(dve, otT_ready[t], b)
                    v = shared[:].rearrange("p (h c) -> p h c", c=32)
                    if t == 0:
                        after(dve, on_made[1], b.ago(1))
                    dve.reciprocal(rc[:, t], v[:, :, DH]).then_inc(rc_made[t], 1)
                    after(dve, rc_made[t], b)
                    after(dve, onT_ready, b.ago(1))
                    dve.tensor_tensor(on[:, t].rearrange("p (h c) -> p h c", c=DH), v[:, :, 0:DH],
                                      rc[:, t].unsqueeze(2).to_broadcast([P, H, DH]), ALU.mult).then_inc(on_made[t], 1)
                if job == "ln_c":
                    after(dve, x4_made, b)
                    stats(x4[:, b.par], 2, lnc_st, lnc_var, b, b.fours)
                if job == "absmax":
                    after(dve, lnc_made, b)
                    dve.tensor_reduce(am[:], on[:], AX_X, ALU.max, apply_absolute_value=True).then_inc(qchain, 1)
                    after4(dve, qchain, b, 1)
                    dve.tensor_scalar(dq[:], am[:], 1e-5, 1.0 / 127.0, ALU.max, ALU.mult).then_inc(qchain, 1)
                    after4(dve, qchain, b, 2)
                    dve.reciprocal(sc[:], dq[:]).then_inc(qchain, 1)
                    after4(dve, th_made[1], b.ago(1), 4)
                    dve.tensor_scalar(ts_[:], dq[:], hgate[:, 0:1], None, ALU.mult).then_inc(qchain, 1)
                    after4(dve, qchain, b, 4)
                    dve.scalar_tensor_tensor(out=hc[:], in0=ts_[:], scalar=wup127[:, 0:1], in1=dq[:],
                                             op0=ALU.mult, op1=ALU.mult).then_inc(qchain2, 1)
                if job == "quant":
                    after(dve, xqa_made, b)
                    after(dve, xqT_ready, b.ago(1))
                    dve.tensor_scalar(xq[:], on[:], MAGIC, 127.0, ALU.subtract, ALU.min).then_inc(xq_made, 1)
                if job == "gate_up":
                    after4(dve, th_made[c % 2], b, c // 2 + 1)
                    if c:
                        after4(dve, hid_made[(c - 1) % 2], b, (c - 1) // 2 + 1)
                    else:
                        after4(dve, hid_made[1], b.ago(1), 4)
                    dve.scalar_tensor_tensor(out=t1[:], in0=th[:], scalar=1.0, in1=shared[:, 0:256],
                                             op0=ALU.add, op1=ALU.mult).then_inc(t1_made[c % 2], 1)
                if job == "h_max":
                    t = c
                    for i in range(2):
                        after4(dve, hid_made[i], b, 2 * (t + 1))
                    dve.tensor_reduce(hm[:, t:t + 1], hid[:, t], AX_X, ALU.max, apply_absolute_value=True).then_inc(hchain[t], 1)
                    after4(dve, hchain[t], b, 1)
                    after(dve, qchain2, b)
                    dve.tensor_scalar(hmc[:, t:t + 1], hm[:, t:t + 1], hc[:, t:t + 1], 1e-5 / 127.0, ALU.mult, ALU.max).then_inc(hchain[t], 1)
                    after4(dve, hchain[t], b, 2)
                    dve.reciprocal(hmr[:, t:t + 1], hmc[:, t:t + 1]).then_inc(hchain[t], 1)
                    after4(dve, hchain[t], b, 3)
                    dve.scalar_tensor_tensor(out=hf[:, t:t + 1], in0=hmr[:, t:t + 1], scalar=127.0, in1=hc[:, t:t + 1],
                                             op0=ALU.mult, op1=ALU.mult).then_inc(hchain[t], 1)
                    dve.tensor_scalar(dqh[:, t:t + 1], hmc[:, t:t + 1], wmean[:, 2:3], None, ALU.mult).then_inc(dqh_made, 1)
                if job == "h_quant":
                    t = c
                    after(dve, hqa_made[t], b)
                    after(dve, hqT_ready[1 - t], b if t else b.ago(1))
                    dve.tensor_scalar(hq[:], hid[:, t], MAGIC, 127.0, ALU.subtract, ALU.min).then_inc(hq_made[t], 1)
                if job == "down":
                    t = c
                    after(dve, dn_ready[t], b)
                    if b.group is None:
                        dve.wait_ge(dqh_made, 2 * b.n + t + 1)
                    else:
                        dve.wait_ge(dqh_made, b.group * 8 + (2 * b.residue + t + 1))
                    dve.scalar_tensor_tensor(out=x4[:, b.par, t], in0=shared[:, 0:D], scalar=dqh[:, t:t + 1],
                                             in1=x4[:, b.par, t], op0=ALU.mult, op1=ALU.add).then_inc(out_made[t], 1)

            pipeline(dve, "dve", work)

        @block.tensor
        def _(pe):
            pe.wait_ge(consts, 5)
            pe.wait_ge(z_made, 1)

            def transposes(b, j, first):
                pe.wait_ge(a_xn, b + 1)
                if not (first and j < 2):
                    pe.wait_ge(a_xt, b - 1)
                for k in range(KT):
                    for t in range(T):
                        ins = pe.transpose(bank[j % 2][:, k * S + t * P:k * S + (t + 1) * P],
                                           xna[:, j % 2, t, k * P:(k + 1) * P], ident[:])
                ins.then_inc(a_xnT, 1)

            def products(b, j, turn, groups):
                pe.wait_ge(ca_ld[j % 4], 16 * turn)
                pe.wait_ge(a_xt, b + 1)
                if j == 0 and groups is not None:
                    pe.wait_ge(a_grp, groups)
                w = z[:, :, P - L0_DH - L0_DH * j:2 * P - L0_DH - L0_DH * j]
                for k in range(KT):
                    first, last = j == 0 and k == 0, j == GROUP - 1 and k == KT - 1
                    pe.matmul(bank[2][:, 0:S], w[:, k], xta[:, j % 2, k],
                              start=first, stop=last)
                    ins = pe.matmul(bank[3][:, 0:S], w[:, k], ca_at(j % 4)[:, k], start=first, stop=last)
                ins.then_inc(a_mm, 1)

            transposes(0, 0, True)
            for b in range(1, GROUP):
                transposes(b, b, True)
                products(b - 1, b - 1, (b - 1) // 4 + 1, None)
            with pe.Fori(1, NG) as g:
                transposes(GROUP * g, 0, False)
                products(GROUP * g - 1, GROUP - 1, 2 * g, None)
                for j in range(1, GROUP):
                    transposes(GROUP * g + j, j, False)
                    products(GROUP * g + (j - 1), j - 1, 2 * g + ((j - 1) // 4 + 1), g)
            products(NB - 1, GROUP - 1, NB // 4, None)

            pe.wait_ge(a_grp, NG)
            for t in range(T):
                for g in range(NG):
                    ins = pe.matmul(bank[t][:, 0:S], k0t[:, g, t * P:(t + 1) * P], q0t[:, g], start=(g == 0), stop=(g == NG - 1))
            ins.then_inc(lagstep, 1)
            for t, v in enumerate((bank[4], maxb)):
                for g in range(NG):
                    ins = pe.transpose(v[:, g * P:(g + 1) * P], k0t[:, g, t * P:(t + 1) * P], ident[:])
            ins.then_inc(v_ready, 1)
            pe.wait_ge(tern, 1)
            pe.matmul(bank[5][:, 0:3], ones[:], wabs[:], start=True, stop=True).then_inc(wsum, 1)
            pe.wait_ge(lag_dma, 16 * 3)
            for t in range(T):
                ins = pe.matmul(bank[2][0:1, 0:S], ones[:, 0:1], lagged[:, t], start=(t == 0), stop=(t == T - 1))
            ins.then_inc(lagstep, 1)
            pe.wait_ge(lag_dma, 16 * 6)
            pe.wait_ge(lagstep, L_W)
            for t in range(T):
                for k in range(T):
                    ins = pe.matmul(bank[t][:, 0:D], circ[:, k, t * P:(t + 1) * P], wout_s[:, k], start=(k == 0), stop=(k == T - 1))
            ins.then_inc(lagstep, 1)
            pe.wait_ge(lagstep, L_WMIX)
            pe.wait_ge(v_made, 1)
            for g in range(NG):
                for k in range(T):
                    ins = pe.matmul(bank[g // 2][:, (g % 2) * D:(g % 2) * D + D], v0[:, k, g * P:(g + 1) * P], wmix[:, k],
                                    start=(k == 0), stop=(k == T - 1))
            ins.then_inc(lagstep, 1)
            pipeline_may_start(pe)

            last = {}

            def use(job, c, b, reader, k=None, each=4):
                bank_name = BANKS[job][c % len(BANKS[job])]
                if bank_name in last:
                    sem_, res, group, k_, each_ = last[bank_name]
                    if b.group is None and group is not None:
                        res, group = res + NB - UNROLL, None
                    elif b.group is not None and group is None:
                        res, group = res - PEEL, b.group
                    was = batch(res, group)
                    if k_ is None:
                        after(pe, sem_, was)
                    elif was.exists:
                        pe.wait_ge(sem_, was.count(k_, each_))
                last[bank_name] = (reader, b.residue, b.group, k, each)

            def work(job, c, b):
                shared = shared_bank(job, c)
                par = b.par
                if job == "norm":
                    t = c
                    if t == 0:
                        after4(pe, ot_made, b, 4)
                    use(job, c, b, on_made[t])
                    for g in range(4):
                        ins = pe.transpose(shared[:, g * P:(g + 1) * P], ot[:, g, t * P:(t + 1) * P], ident[:])
                    ins.then_inc(otT_ready[t], 1)
                if job == "norm_T":
                    after(pe, on_made[1], b)
                    use(job, c, b, otn_made)
                    for k in range(KT):
                        for t in range(T):
                            ins = pe.transpose(shared[:, k * S + t * P:k * S + (t + 1) * P], on[:, t, k * P:(k + 1) * P], ident[:])
                    ins.then_inc(onT_ready, 1)
                if job == "o":
                    after(pe, otn_made, b)
                    use(job, c, b, o_out)
                    for t in range(T):
                        for k in range(KT):
                            ins = pe.matmul(shared[:, t * D:(t + 1) * D], otn[:, k, t * P:(t + 1) * P], wo[:, k], start=(k == 0), stop=(k == KT - 1))
                    ins.then_inc(op_ready, 1)
                if job == "quant_T":
                    after(pe, xq_made, b)
                    use(job, c, b, xqt_made)
                    v = shared[:, 0:S].bitcast(BF16)
                    for k in range(KT):
                        for t in range(T):
                            ins = pe.transpose(v[:, k * S + t * P:k * S + (t + 1) * P], xq[:, t, k * P:(k + 1) * P], identb[:])
                    ins.then_inc(xqT_ready, 1)
                if job == "exp":
                    s = c
                    u, key = s // 2, (s // 2) % 2
                    if s == 0:
                        landed(pe, mx_ld, b, 32)
                        after4(pe, ex_made[3], b.ago(1), 4)
                    else:
                        after4(pe, ex_made[(s - 1) % 4], b, (s - 1) // 4 + 1)
                    for j in range(2):
                        h = 4 * (u // 2) + 2 * (s % 2) + j
                        ins = pe.matmul(cbank[:, j * S:(j + 1) * S], ks[par][0:AROWS, h, key * P:(key + 1) * P],
                                        qs[par][0:AROWS, h, :], start=True, stop=True)
                    ins.then_inc(sc_ready[s % 4], 1)
                if job == "pv":
                    u = c
                    g, key = u // 2, u % 2
                    for i in (2 * u, 2 * u + 1):
                        after4(pe, ex_made[i % 4], b, i // 4 + 1)
                    if u == 0:
                        after(pe, va_made, b)
                        after4(pe, ot_made, b.ago(1), 4)
                    elif key == 0:
                        after4(pe, ot_made, b, g)
                    for i in range(4):
                        ins = pe.matmul(obank[32 * i:32 * i + 32, 0:S],
                                        va[:, par, key, (4 * g + i) * 32:(4 * g + i) * 32 + 32],
                                        pt[:, (2 * u + i // 2) % 4, i % 2], start=(key == 0), stop=(key == 1))
                    ins.then_inc(pv_done[u % 2], 1)
                if job == "gate_up":
                    t, n = c // 4, c % 4
                    if c == 0:
                        after(pe, xqt_made, b)
                    use(job, c, b, t1_made[c % 2], c // 2 + 1)
                    for i, w in enumerate((wg, wu)):
                        for k in range(KT):
                            ins = pe.matmul(shared[:, i * 256:(i + 1) * 256], xqt[:, k, t * P:(t + 1) * P],
                                            w[:, k, n * 256:(n + 1) * 256], start=(k == 0), stop=(k == KT - 1))
                    ins.then_inc(gu_ready[c % 2], 1)
                if job == "h_T":
                    t = c
                    after(pe, hq_made[t], b)
                    use(job, c, b, hqt_made[t])
                    v = shared[:, :].bitcast(BF16)
                    for k in range(IC):
                        ins = pe.transpose(v[:, k * P:(k + 1) * P], hq[:, k * P:(k + 1) * P], identb[:])
                    ins.then_inc(hqT_ready[t], 1)
                if job == "down":
                    t = c
                    after(pe, hqt_made[t], b)
                    use(job, c, b, out_made[t])
                    for k in range(IC):
                        ins = pe.matmul(shared[:, 0:D], hqt[:, k], wd[:, k], start=(k == 0), stop=(k == IC - 1))
                    ins.then_inc(dn_ready[t], 1)
                if job == "max":
                    p, t = c // 2, c % 2
                    if c == 0:
                        landed(pe, qs_ld, b, 48)
                        landed(pe, ks_ld, b, 64)
                    use(job, c, b, mx_made[t], p + 1, 8)
                    for j in range(2):
                        h = 2 * p + j
                        ins = pe.matmul(shared[:, j * S:(j + 1) * S], qs[par][0:QROWS, h, t * P:(t + 1) * P],
                                        ks[par][0:QROWS, h, :], start=True, stop=True)
                    ins.then_inc(mx_ready[t], 1)
                if job == "max_T":
                    for t in range(T):
                        after8(pe, mx_made[t], b, 8)
                    use(job, c, b, nml_made)
                    for t in range(T):
                        ins = pe.transpose(shared[0:H, t * P:(t + 1) * P], mx[:, t, :], ident[:])
                    ins.then_inc(mxT_ready, 1)
                if job == "xT_b":
                    after(pe, xnb_made, b)
                    use(job, c, b, xbt_made)
                    for k in range(KT):
                        for t in range(T):
                            ins = pe.transpose(shared[:, k * S + t * P:k * S + (t + 1) * P], xn[:, t, k * P:(k + 1) * P], ident[:])
                    ins.then_inc(xnb_T, 1)
                if job == "q":
                    after(pe, xbt_made, b)
                    use(job, c, b, qh_made)
                    for m in range(KT):
                        for k in range(KT):
                            ins = pe.matmul(shared[:, m * S:(m + 1) * S], wq[:, k, m * P:(m + 1) * P], xbt[:, k], start=(k == 0), stop=(k == KT - 1))
                    ins.then_inc(qp_ready, 1)
                if job == "v":
                    use(job, c, b, va_made)
                    for t in range(T):
                        for k in range(KT):
                            ins = pe.matmul(shared[:, t * D:(t + 1) * D], ct[:, par, k, t * P:(t + 1) * P], wv[:, k], start=(k == 0), stop=(k == KT - 1))
                    ins.then_inc(vp_ready, 1)
                if job == "xT_a":
                    after(pe, xna_made, b)
                    use(job, c, b, xal_made)
                    for k in range(KT):
                        for t in range(T):
                            ins = pe.transpose(shared[:, k * S + t * P:k * S + (t + 1) * P], xn[:, t, k * P:(k + 1) * P], ident[:])
                    ins.then_inc(xna_T, 1)
                if job == "route":
                    after(pe, xal_made, b)
                    use(job, c, b, lt_made)
                    ops = [(w, v, k) for w, v in ((rwh, xah), (rwl, xah), (rwh, xal)) for k in range(KT)]
                    for i, (w, v, k) in enumerate(ops):
                        ins = pe.matmul(shared[:, 0:S], w[:, k], v[:, k], start=(i == 0), stop=(i == len(ops) - 1))
                    ins.then_inc(rt_ready, 1)
                if job == "routeT":
                    after(pe, lt_made, b)
                    use(job, c, b, rchain, 1)
                    apart(pe, parted)
                    for t in range(T):
                        ins = pe.transpose(shared[:, t * NE:(t + 1) * NE], lt[:, t * P:(t + 1) * P], ident[0:NE, 0:NE])
                    ins.then_inc(rtt_ready, 1)
                if job == "gateT":
                    after4(pe, rchain2, b, 4)
                    use(job, c, b, gt_made)
                    for t in range(T):
                        ins = pe.transpose(shared[0:NE, t * P:(t + 1) * P], gg[:, t], ident[:])
                    ins.then_inc(gT_ready, 1)
                if job == "gbias":
                    after(pe, gt_made, b)
                    use(job, c, b, gb_out)
                    for t in range(T):
                        ins = pe.matmul(shared[:, t * D:(t + 1) * D], gt[:, t * P:(t + 1) * P], eb_s[:], start=True, stop=True)
                    ins.then_inc(gb_ready, 1)
                if job == "k":
                    landed(pe, c_ld, b, 16)
                    use(job, c, b, kf_made)
                    for m in range(KT):
                        for k in range(KT):
                            ins = pe.matmul(shared[:, m * S:(m + 1) * S], wk[:, k, m * P:(m + 1) * P], ct[:, par, k], start=(k == 0), stop=(k == KT - 1))
                    ins.then_inc(kp_ready, 1)
                if job == "expert":
                    t, p = c % 2, c // 2
                    if p:
                        after4(pe, e_tmp[t], b, p)
                    else:
                        after4(pe, e_tmp[t], b.ago(1), 4)
                    ops = [(v, w, k) for v, w in ((xah, ewh), (xah, ewl), (xal, ewh)) for k in range(KT)]
                    for i, (v, w, k) in enumerate(ops):
                        ins = pe.matmul(ebank[t][:, :], v[:, k, t * P:(t + 1) * P], w[:, k, p * 512:(p + 1) * 512],
                                        start=(i == 0), stop=(i == len(ops) - 1))
                    ins.then_inc(e_ready[t], 1)

            pipeline(pe, "pe", work)


def kernel(x, ctx_1024, mask_Bx1xS2_ik0, L0_xattn_Wq, L0_xattn_bq, L0_xattn_Wout, L0_xattn_bout,
           L0_ffn_router_w, L0_ffn_router_b, L0_ffn_expert_w, L0_ffn_expert_b, L1_xattn_Wq, L1_xattn_bq,
           L1_xattn_Wk, L1_xattn_bk, L1_xattn_Wv, L1_xattn_bv, L1_xattn_Wo, L1_xattn_bo, L1_ffn_w_gate,
           L1_ffn_w_up, L1_ffn_w_down):
    import numpy as np
    import concourse.bacc as bacc
    from concourse.bass_utils import run_bass_kernel_spmd

    arrays = {
        "x": np.asarray(x),
        "ctxT": np.asarray(ctx_1024).transpose(0, 2, 1),
        "mask": np.asarray(mask_Bx1xS2_ik0).reshape(NB, S),
        "wq0": np.asarray(L0_xattn_Wq),
        "bq0": np.asarray(L0_xattn_bq),
        "wout_r": np.asarray(L0_xattn_Wout)[::-1],
        "bout": np.asarray(L0_xattn_bout),
        "rwT": np.asarray(L0_ffn_router_w).T,
        "rb": np.asarray(L0_ffn_router_b),
        "ewT": np.asarray(L0_ffn_expert_w).transpose(2, 0, 1).reshape(D, NE * D),
        "eb": np.asarray(L0_ffn_expert_b),
        "wqT": np.asarray(L1_xattn_Wq).T,
        "bq": np.asarray(L1_xattn_bq).reshape(KT, P).T,
        "wkT": np.asarray(L1_xattn_Wk).T,
        "bk": np.asarray(L1_xattn_bk).reshape(KT, P).T,
        "wvT": np.asarray(L1_xattn_Wv).T,
        "bv": np.asarray(L1_xattn_bv),
        "woT": np.asarray(L1_xattn_Wo).T,
        "bo": np.asarray(L1_xattn_bo),
        "wgT": np.asarray(L1_ffn_w_gate).T,
        "wuT": np.asarray(L1_ffn_w_up).T,
        "wdT": np.asarray(L1_ffn_w_down).T,
    }
    arrays = {f"in_{name}": np.ascontiguousarray(a) for name, a in arrays.items()}
    nc = bacc.Bacc("TRN2", target_bir_lowering=False, num_devices=1)
    args = [nc.dram_tensor(name, a.shape, mybir.dt.from_np(a.dtype), kind="ExternalInput").ap()
            for name, a in arrays.items()]
    args.append(nc.dram_tensor("out", (NB, S, D), F32, kind="ExternalOutput").ap())
    build(nc, *args)
    result = run_bass_kernel_spmd(nc, [arrays], core_ids=[0])
    return result.results[0]["out"]
```
